# Optimizing a Trainium2 kernel written in Bass

```python
import numpy as np
import jax
import jax.numpy as jnp

def _softmax(x, axis=-1):
    return jax.nn.softmax(x, axis=axis)

def _gelu(x):
    return jax.nn.gelu(x, approximate=True)

def _silu(x):
    return jax.nn.silu(x)

def _sigmoid(x):
    return jax.nn.sigmoid(x)

def _layernorm(x, axis=-1, eps=1e-05):
    m = jnp.mean(x, axis=axis, keepdims=True)
    v = jnp.var(x, axis=axis, keepdims=True)
    return (x - m) / jnp.sqrt(v + eps)

def _scatter_add(tgt, idx, src, axis=0):
    return tgt.at[idx].add(src)

def _segment_sum(src, seg, n):
    return jax.ops.segment_sum(src, seg, n)
kernel_name = 'mk_recurrent_d1_jaxref_r4_265dea'

def setup_inputs(seed: int=0):
    np.random.seed(seed)
    _w = jnp.asarray

    def _L0_attn_setup():
        import jax, jax.numpy as jnp
        import numpy as np
        HEADS = 16

        def fenwick_mask(T):
            m = np.zeros((T, T), dtype=bool)
            for i in range(T):
                j = i + 1
                while j <= T:
                    m[i, j - 1] = True
                    j += j & -j
                step = 1
                while i - step >= 0:
                    m[i, i - step] = True
                    step *= 2
            m &= np.tril(np.ones((T, T), dtype=bool))
            return jnp.asarray(m)
        key = jax.random.key(seed)
        ks = jax.random.split(key, 4)
        B, T, C = (2, 512, 256)
        x = jax.random.normal(ks[0], (B, T, C), dtype=jnp.float32)
        W_qkv = jax.random.normal(ks[1], (C, 3 * C), dtype=jnp.float32) * C ** (-0.5)
        b_qkv = jnp.zeros((3 * C,), dtype=jnp.float32)
        W_proj = jax.random.normal(ks[2], (C, C), dtype=jnp.float32) * C ** (-0.5)
        b_proj = jnp.zeros((C,), dtype=jnp.float32)
        return {'x': x, 'W_qkv': W_qkv, 'b_qkv': b_qkv, 'W_proj': W_proj, 'b_proj': b_proj}
    _L0_attn_in = _L0_attn_setup()

    def _L0_ffn_setup():
        import jax, jax.numpy as jnp
        import numpy as np
        DIM = 256
        HID = 256
        N_ROUTED = 7
        N_SHARED = 1
        TOP_K = 2
        B, S = (4, 512)
        key = jax.random.key(seed)
        ks = jax.random.split(key, 8)
        sc = 0.02
        return {'x': jax.random.normal(ks[0], (B, S, DIM), jnp.float32), 'gate_w': jax.random.normal(ks[1], (N_ROUTED, DIM), jnp.float32) * sc, 'expert_bias': jnp.zeros((N_ROUTED,), jnp.float32), 'sw1': jax.random.normal(ks[2], (DIM, HID), jnp.float32) * sc, 'sb1': jnp.zeros((HID,), jnp.float32), 'sw2': jax.random.normal(ks[3], (HID, DIM), jnp.float32) * sc, 'sb2': jnp.zeros((DIM,), jnp.float32), 'rw1': jax.random.normal(ks[4], (N_ROUTED, DIM, HID), jnp.float32) * sc, 'rb1': jnp.zeros((N_ROUTED, HID), jnp.float32), 'rw2': jax.random.normal(ks[5], (N_ROUTED, HID, DIM), jnp.float32) * sc, 'rb2': jnp.zeros((N_ROUTED, DIM), jnp.float32)}
    _L0_ffn_in = _L0_ffn_setup()
    _d = {'L0_attn_x': _L0_attn_in['x'], 'L0_attn_W_qkv': _L0_attn_in['W_qkv'], 'L0_attn_b_qkv': _L0_attn_in['b_qkv'], 'L0_attn_W_proj': _L0_attn_in['W_proj'], 'L0_attn_b_proj': _L0_attn_in['b_proj'], 'L0_ffn_gate_w': _L0_ffn_in['gate_w'], 'L0_ffn_expert_bias': _L0_ffn_in['expert_bias'], 'L0_ffn_sw1': _L0_ffn_in['sw1'], 'L0_ffn_sb1': _L0_ffn_in['sb1'], 'L0_ffn_sw2': _L0_ffn_in['sw2'], 'L0_ffn_sb2': _L0_ffn_in['sb2'], 'L0_ffn_rw1': _L0_ffn_in['rw1'], 'L0_ffn_rb1': _L0_ffn_in['rb1'], 'L0_ffn_rw2': _L0_ffn_in['rw2'], 'L0_ffn_rb2': _L0_ffn_in['rb2']}
    _x0 = _d['L0_attn_x']
    _d['L0_attn_x'] = jax.random.normal(jax.random.fold_in(jax.random.key(seed), 1), (8, 512, 256), dtype=_x0.dtype)
    del _x0
    return _d

def reference(L0_attn_x, L0_attn_W_qkv, L0_attn_b_qkv, L0_attn_W_proj, L0_attn_b_proj, L0_ffn_gate_w, L0_ffn_expert_bias, L0_ffn_sw1, L0_ffn_sb1, L0_ffn_sw2, L0_ffn_sb2, L0_ffn_rw1, L0_ffn_rb1, L0_ffn_rw2, L0_ffn_rb2):

    def _L0_attn_ref(x, W_qkv, b_qkv, W_proj, b_proj):
        import jax, jax.numpy as jnp
        import numpy as np
        HEADS = 16

        def fenwick_mask(T):
            m = np.zeros((T, T), dtype=bool)
            for i in range(T):
                j = i + 1
                while j <= T:
                    m[i, j - 1] = True
                    j += j & -j
                step = 1
                while i - step >= 0:
                    m[i, i - step] = True
                    step *= 2
            m &= np.tril(np.ones((T, T), dtype=bool))
            return jnp.asarray(m)
        B, T, C = x.shape
        H = HEADS
        Dh = C // H
        scale = Dh ** (-0.5)
        qkv = (x @ W_qkv + b_qkv).reshape(B, T, 3, H, Dh)
        qkv = jnp.transpose(qkv, (2, 0, 3, 1, 4))
        q, k, v = (qkv[0], qkv[1], qkv[2])
        attn = jnp.einsum('bhtd,bhsd->bhts', q, k) * scale
        mask = fenwick_mask(T)
        attn = jnp.where(mask[None, None], attn, -jnp.inf)
        attn = jax.nn.softmax(attn, axis=-1)
        out = jnp.einsum('bhts,bhsd->bhtd', attn, v)
        out = jnp.transpose(out, (0, 2, 1, 3)).reshape(B, T, C)
        return out @ W_proj + b_proj

    def _L0_ffn_ref(x, gate_w, expert_bias, sw1, sb1, sw2, sb2, rw1, rb1, rw2, rb2):
        import jax, jax.numpy as jnp
        import numpy as np
        DIM = 256
        HID = 256
        N_ROUTED = 7
        N_SHARED = 1
        TOP_K = 2
        B, S = (4, 512)
        b, s, d = x.shape
        xf = x.reshape(-1, d)
        sh = jax.nn.gelu(xf @ sw1 + sb1, approximate=False) @ sw2 + sb2
        sh = sh / N_SHARED
        logits = xf @ gate_w.T + jax.lax.stop_gradient(expert_bias)
        topv, topi = jax.lax.top_k(logits, TOP_K)
        w = jax.nn.softmax(topv, axis=-1)
        combine = jnp.sum(jax.nn.one_hot(topi, N_ROUTED, dtype=xf.dtype) * w[..., None], axis=1)
        h = jax.nn.gelu(jnp.einsum('td,edh->eth', xf, rw1) + rb1[:, None, :], approximate=False)
        out_e = jnp.einsum('eth,ehd->etd', h, rw2) + rb2[:, None, :]
        routed = jnp.einsum('te,etd->td', combine, out_e)
        return (sh + routed).reshape(b, s, d)
    x = L0_attn_x
    xn = _layernorm(x, axis=-1)
    s = _L0_attn_ref(xn, L0_attn_W_qkv, L0_attn_b_qkv, L0_attn_W_proj, L0_attn_b_proj)
    g = _silu(_L0_ffn_ref(xn, L0_ffn_gate_w, L0_ffn_expert_bias, L0_ffn_sw1, L0_ffn_sb1, L0_ffn_sw2, L0_ffn_sb2, L0_ffn_rw1, L0_ffn_rb1, L0_ffn_rw2, L0_ffn_rb2))
    x = x + s * g
    return x

_drawn_inputs = setup_inputs


def setup_inputs(seed=0):
    import zlib

    import numpy as np

    out = dict(_drawn_inputs(seed))
    spreads = {'L0_attn_b_qkv': (0.0, 0.8),
     'L0_attn_b_proj': (0.0, 0.8),
     'L0_ffn_expert_bias': (0.0, 0.699),
     'L0_ffn_sb1': (0.0, 0.8),
     'L0_ffn_sb2': (0.0, 0.307),
     'L0_ffn_rb1': (0.0, 0.8),
     'L0_ffn_rb2': (0.0, 0.451)}
    factors = {'L0_ffn_gate_w': 3.374,
     'L0_ffn_sw1': 4.221,
     'L0_ffn_sw2': 3.936,
     'L0_ffn_rw1': 5.871,
     'L0_ffn_rw2': 5.484}
    for name, (base, spread) in spreads.items():
        noise = np.random.default_rng([zlib.crc32(name.encode()), seed]).standard_normal(out[name].shape)
        drawn = base * np.exp(spread * noise) if base else spread * noise
        out[name] = jnp.asarray(drawn.astype(out[name].dtype))
    for name, factor in factors.items():
        out[name] = (out[name] * factor).astype(out[name].dtype)
    return out
```

```python
from contextlib import ExitStack

import numpy as np

import concourse.bass as bass
from concourse import mybir

F32 = mybir.dt.float32
F32R = mybir.dt.float32r
U32 = mybir.dt.uint32
I32 = mybir.dt.int32
ALU = mybir.AluOpType
ACT = mybir.ActivationFunctionType
AX = mybir.AxisListType

P = 128
B, T, C = 8, 512, 256
HEADS = 16
DH = C // HEADS
TT = T // P
NT = B * TT
CH = C // P
HH = HEADS // CH
DIST = [0] + [1 << k for k in range(T.bit_length() - 1)]
ND = len(DIST)
E = 7
SHARED = E
EPS = 1e-5
SCALE = DH ** -0.5
ROW = C + 2
BLIND = 2
TILES_B = 12
RT = (B - BLIND) * TILES_B
SLOTS = RT * P
TAIL = SLOTS // P - 2 * NT
FAR = 1.0e6
SECOND = ND - 8
RING = 4
assert RT >= 2 * NT + E - 1 and 128 * 8 == P * 8

CONST = {}
_at = 0
for _name, _n in (("ident", P), ("head_sum", HH), ("mask", TT * ND), ("before", P), ("ones", P),
                  ("edges", NT), ("tile_no", RT), ("lane", 1), ("rank0", E), ("expert", E),
                  ("token2", NT), ("row_expert", 1), ("row_hi", 1), ("row_lo", 1), ("tail", TAIL),
                  ("minus_half", TT)):
    CONST[_name] = (_at, _n)
    _at += _n
NCONST = _at


def constants():
    c = np.zeros((P, NCONST), np.float32)
    p = np.arange(P)

    def put(name, v):
        at, n = CONST[name]
        c[:, at:at + n] = np.broadcast_to(np.asarray(v, np.float32), (P, n))

    put("ident", np.eye(P))
    put("head_sum", (p[:, None] // DH == np.arange(HH)[None, :]))
    tok = np.arange(TT)[None, :, None] * P + p[:, None, None]
    put("mask", np.where(tok >= np.array(DIST)[None, None, :], 0.0, -1e30).reshape(P, -1))
    put("before", p[:, None] < p[None, :])
    put("ones", np.ones((1, P)))
    put("edges", np.arange(NT)[None] * P)
    put("tile_no", np.arange(RT)[None])
    put("lane", p[:, None])
    put("rank0", (E - 1 - np.arange(E))[None])
    put("expert", np.arange(E)[None])
    put("token2", 2 * (np.arange(NT)[None] * P + p[:, None]))
    put("row_expert", np.where(p < 2 * E, p % E, -1)[:, None])
    put("row_hi", ((p < E) | (p == 2 * E))[:, None])
    put("row_lo", (((p >= E) & (p < 2 * E)) | (p == 2 * E + 1))[:, None])
    put("tail", np.arange(TAIL)[None] * P + p[:, None])
    put("minus_half", np.full((1, TT), -0.5))
    s = np.zeros((8, 2, HH, 8, P), np.float32)
    for d in range(8):
        for ch in range(P):
            s[d, :, ch // DH, d, ch] = 1.0
    return c, s.reshape(P, 8 * P)


def batch_plan(routed):
    steps = []
    for i in range(TILES_B + 3 if routed else 0):
        steps += [("down", i - 3)] if 0 <= i - 3 < TILES_B else []
        steps += [("th", i - 2)] if 0 <= i - 2 < TILES_B else []
        steps += [("up", i - 1)] if 0 <= i - 1 < TILES_B else []
        steps += [("tx", i)] if i < TILES_B else []
    plan = [("split", 0)] + [("qkv", i) for i in range(3)] + [("product", 0), ("product_rest", 0)]
    plan += [("qkv", i) for i in range(3, 6)]
    plan += [("shared_up", 0), ("shared_up", 1)]
    plan += [("scores", 0), ("product", 1), ("soft_max", 0)]
    plan += steps[:9]
    plan += [("shared_down", 0), ("shared_down", 1)]
    plan += [("product_rest", 1), ("scores", 1), ("soft_norm", 0), ("turn", 0), ("soft_max", 1)]
    steps = steps[9:]
    rest = max(0, len(steps) - 2 * ND)
    for h in range(CH):
        for i in range(ND):
            plan += [("pv", h * ND + i)]
            if h == 0 and i == 0:
                plan += [("soft_norm", 1), ("turn", 1)]
            plan += steps[:1]
            steps = steps[1:]
    plan += [("mix_split", 0)] + steps + [("project", 0), ("project", 1)]
    return plan


USE = {}
for _s in [s for s in batch_plan(False)]:
    for _ in range(2 if _s[0] == "turn" else 1 if _s[0] in ("qkv", "shared_up", "shared_down", "pv", "project") else 0):
        USE.setdefault(_s, []).append(sum(map(len, USE.values())))
USES = sum(map(len, USE.values()))
BANKS = 3
assert USES % BANKS == 0
BANK_USES = USES // BANKS


def build(nc, x, w_qkv, b_qkv, w_proj, bias_rows, gate_t, expert_bias, w1, w2, sb1, consts, spread,
          out, slots_dram, routed_dram, shared_dram):
    x_b = x.rearrange("b (t p) c -> b p t c", p=P)
    out_b = out.rearrange("b (t p) c -> b p t c", p=P)
    shared_b = shared_dram.rearrange("(b t p) c -> b p t c", p=P, t=TT)
    routed_b = routed_dram.rearrange("(b t p k) c -> b p t (k c)", p=P, t=TT, k=2)
    slots_t = slots_dram.rearrange("(j p) c -> j p c", p=P)

    with ExitStack() as ctx:
        def sb(name, shape, dt=F32):
            return ctx.enter_context(nc.sbuf_tensor(name, shape, dt))

        def bank(name):
            return ctx.enter_context(nc.psum_tensor(name, [P, 512], F32))

        def sem(name):
            return ctx.enter_context(nc.semaphore(name))

        rows = sb("rows", [P, NT, ROW])
        xnt = sb("xnt", [P, B, CH * T])
        wqkv_h, wqkv_l = sb("wqkv_h", [P, CH, 3 * C], F32R), sb("wqkv_l", [P, CH, 3 * C], F32R)
        wp_h, wp_l = sb("wp_h", [P, CH, C], F32R), sb("wp_l", [P, CH, C], F32R)
        w1_h, w1_l = sb("w1_h", [P, E + 1, CH, C], F32R), sb("w1_l", [P, E + 1, CH, C], F32R)
        w2_h, w2_l = sb("w2_h", [P, E + 1, CH, C], F32R), sb("w2_l", [P, E + 1, CH, C], F32R)
        sp_r = sb("sp_r", [P, 8, P], F32R)
        cst = sb("cst", [P, NCONST])
        bqkv = sb("bqkv", [P, 6])
        bs1 = sb("bs1", [P, CH])
        gate = sb("gate", [P, CH, E])
        ebias = sb("ebias", [P, E])
        brow = sb("brow", [16, 2 * C], F32R)
        dense_pick = sb("dense_pick", [16, P], F32R)
        t_h, t_l = sb("t_h", [P, CH, T], F32R), sb("t_l", [P, CH, T], F32R)
        qkv = sb("qkv", [P, 6, T])
        prod = sb("prod", [P, RING, T])
        part = sb("part", [P, 2, T])
        acc = sb("acc", [P, CH, T])
        sco = sb("sco", [P, TT, ND, HH])
        prb = sb("prb", [P, TT, ND, HH])
        phl = sb("phl", [P, TT, ND, 2, HH], F32R)
        red = sb("red", [P, 3, TT, HH])
        turned = sb("turned", [P, CH, 2, T], F32R)
        xs = sb("xs", [P, 2, ROW])
        xs_h, xs_l = sb("xs_h", [P, CH, P], F32R), sb("xs_l", [P, CH, P], F32R)
        hr = sb("hr", [P, C])
        hr_h, hr_l = sb("hr_h", [P, CH, P], F32R), sb("hr_l", [P, CH, P], F32R)
        ys = sb("ys", [P, 2, C])
        pick = sb("pick", [16, 4, P], F32R)
        home = sb("home", [P, 4], U32)
        homef = sb("homef", [P, 2])
        lg = part[:].rearrange("p a b -> p (a b)")[:, 0:NT * E].rearrange("p (t e) -> p t e", e=E)
        weight = sb("weight", [P, 2, NT])
        where = sb("where", [P, 2, NT], U32)
        where_pad = sb("where_pad", [P, E + TAIL], U32)
        tile_ef = sb("tile_ef", [P, RT])
        tile_ei = sb("tile_ei", [1, RT], I32)
        tile_row = sb("tile_row", [16, RT])
        stats = sb("stats", [P, TT, 6])
        mv = sb("mv", [P, TT, 2])
        rstd = sb("rstd", [P, 2, TT])

        def k(name):
            at, n = CONST[name]
            return cst[:, at:at + n]

        ident = k("ident")
        qf = qkv[:].rearrange("p a b -> p (a b)")
        rk = [qf[:, 1024 + i * 256:1024 + (i + 1) * 256] for i in range(8)]
        
        xt_f = qkv[:, 0:CH, :]
        xr = acc[:].rearrange("p c (t n) -> p (c t) n", n=C)
        sh_out = xr
        hs = acc
        zpad = xs[:, 0, :]

        bank_d = [bank(f"bank_d{i}") for i in range(BANKS)]
        bank_s, bank_tx, bank_up, bank_th, bank_down = map(
            bank, ("bank_s", "bank_tx", "bank_up", "bank_th", "bank_down"))

        x_in = [sem(f"x_in{i}") for i in range(B)]
        small_in = sem("small_in")
        raw_in = [sem(f"raw_in{i}") for i in range(RING)]
        hi_made, lo_made = sem("hi_made"), sem("lo_made")
        mv_done, rstd_done, pool_ve = sem("mv_done"), sem("rstd_done"), sem("pool_ve")
        xr_done, rows_done = sem("xr_done"), sem("rows_done")
        t_done, xt_done = sem("t_done"), sem("xt_done")
        logit_done, lg_done = sem("logit_done"), sem("lg_done")
        brow_done, brow_in = sem("brow_done"), sem("brow_in")
        rank_done, count_done, gap_done, exp_done = map(sem, ("rank_done", "count_done", "gap_done", "exp_done"))
        route_done, pad_done = sem("route_done"), sem("pad_done")
        scattered = sem("scattered")
        d_full = [sem(f"d_full{i}") for i in range(BANKS)]
        d_free = [sem(f"d_free{i}") for i in range(BANKS)]
        split_h, split_l = sem("split_h"), sem("split_l")
        prod_ready, prod_used = sem("prod_ready"), sem("prod_used")
        s_free = sem("s_free")
        shifted, exped, normed, p_h, p_l = map(sem, ("shifted", "exped", "normed", "p_h", "p_l"))
        part_added = sem("part_added")
        mix_h, mix_l = sem("mix_h"), sem("mix_l")
        hs_h, hs_l = sem("hs_h"), sem("hs_l")
        sh_stored = sem("sh_stored")
        xs_in = [sem("xs_in0"), sem("xs_in1")]
        tx_done, xs_hi, xs_lo = sem("tx_done"), sem("xs_hi"), sem("xs_lo")
        up_done, gelu_done = sem("up_done"), sem("gelu_done")
        th_done, hr_hi, hr_lo = sem("th_done"), sem("hr_hi"), sem("hr_lo")
        down_done, y_made = sem("down_done"), sem("y_made")
        y_out = [sem("y_out0"), sem("y_out1")]
        home_f, home_done, pick_done = sem("home_f"), sem("home_done"), sem("pick_done")
        dve_done = sem("dve_done")
        act_turn, pool_turn, dve_turn, sp_turn = map(sem, ("act_turn", "pool_turn", "dve_turn", "sp_turn"))
        c_in = [sem("c_in0"), sem("c_in1")]
        g_parts, silu_done, sg_done, o_made = sem("g_parts"), sem("silu_done"), sem("sg_done"), sem("o_made")
        c_out = [sem("c_out0"), sem("c_out1")]

        def chunk_list():
            wq = w_qkv.rearrange("(c p) n -> p c n", p=P)
            for h in range(3):
                yield (wq[:, :, h * C:(h + 1) * C], wqkv_h[:, :, h * C:(h + 1) * C], wqkv_l[:, :, h * C:(h + 1) * C])
            for h in range(2):
                yield (spread[:, h * 512:(h + 1) * 512], sp_r[:, 4 * h:4 * h + 4, :], None)
            yield (w_proj.rearrange("(c p) n -> p c n", p=P), wp_h[:], wp_l[:])
            for e in [SHARED] + list(range(E)):
                yield (w1[e].rearrange("(c p) n -> p c n", p=P), w1_h[:, e], w1_l[:, e])
                yield (w2[e].rearrange("(c p) n -> p c n", p=P), w2_h[:, e], w2_l[:, e])

        chunks = list(chunk_list())
        NCH = len(chunks)
        EARLY = 8

        def staged(n, like):
            a = prod[:, n % RING, :]
            return a.rearrange("p (c n) -> p c n", c=like.shape[1]) if len(like.shape) == 3 else a

        def hold(eng, turn, s, v):
            eng.wait_ge(s, v)
            if turn is not None and not isinstance(v, int):
                eng.sem_inc(turn, 1)

        def drained(eng, turn, b, use):
            hold(eng, turn, d_free[use % BANKS], b * BANK_USES + use // BANKS + 2)

        def use_of(kind, i, j=0):
            return USE[kind, i][j]

        def comb(n):
            f = rows[:].rearrange("p a b -> p (a b)")[:, n * 4096:(n + 1) * 4096]
            return (f[:, 0:1024].rearrange("p (t c) -> p t c", c=C),
                    f[:, 1024:2048].rearrange("p (t c) -> p t c", c=C),
                    f[:, 2048:4096].rearrange("p (t c) -> p t c", c=2 * C))

        block = ctx.enter_context(nc.Block())

        @block.sync
        def _(sp):
            for b in range(2):
                sp.dma_start(rows[:, b * TT:(b + 1) * TT, 0:C], x_b[b]).then_inc(x_in[b], 16)
            sp.dma_start(cst[:], consts).then_inc(small_in, 16)
            sp.dma_start(bqkv[:], b_qkv).then_inc(small_in, 16)
            sp.dma_start(bs1[:], sb1).then_inc(small_in, 16)
            sp.dma_start(gate[:], gate_t.rearrange("(c p) e -> p c e", p=P)).then_inc(small_in, 16)
            sp.dma_start(ebias[:], expert_bias.rearrange("(a e) -> a e", a=1).to_broadcast([P, E])).then_inc(small_in, 16)
            sp.dma_start(sco[0:16].rearrange("p a b c -> p (a b c)")[:, 0:256], bias_rows[:, 0:C]).then_inc(brow_in, 16)
            sp.dma_start(prb[0:16].rearrange("p a b c -> p (a b c)")[:, 0:256], bias_rows[:, C:2 * C]).then_inc(brow_in, 16)
            for b in range(2, B):
                sp.dma_start(rows[:, b * TT:(b + 1) * TT, 0:C], x_b[b]).then_inc(x_in[b], 16)
            for n, (src, hi, lo) in enumerate(chunks):
                if n >= RING:
                    sp.wait_ge(lo_made, n - RING + 1)
                sp.dma_start(staged(n, src), src).then_inc(raw_in[n % RING], 16)

            with sp.Fori(0, BLIND) as b:
                for i in range(2):
                    drained(sp, sp_turn, b, use_of("shared_down", i))
                sp.dma_start(shared_b[bass.ds(b, 1)].rearrange("a p t c -> p (a t) c"), sh_out).then_inc(sh_stored, 16)
            sp.wait_ge(scattered, 16 * (2 * NT + E + TAIL - 4))
            for n in range(2):
                sp.wait_ge(y_out[n], 32)
            with sp.Fori(BLIND, B) as b:
                for kind, i in batch_plan(True):
                    if kind == "tx":
                        m = (b - BLIND) * TILES_B + i
                        hold(sp, sp_turn, tx_done, m + 1)
                        hold(sp, sp_turn, home_done, m + 1)
                        sp.dma_start(xs[:, i % 2, :], slots_t[bass.ds(m, 1)].rearrange("a p c -> p (a c)"))\
                            .then_inc(xs_in[i % 2], 16)
                    if kind == "shared_down" and i == 1:
                        for j in range(2):
                            drained(sp, sp_turn, b, use_of("shared_down", j))
                        sp.dma_start(shared_b[bass.ds(b, 1)].rearrange("a p t c -> p (a t) c"), sh_out)\
                            .then_inc(sh_stored, 16)

            sp.wait_ge(sh_stored, 16 * (B + 1))
            for n in range(2):
                sp.wait_ge(y_out[n], 16 * (RT // 2 + 2))
            with sp.Fori(0, B // 2) as g:
                for n in range(2):
                    hold(sp, sp_turn, c_out[n], g * 16 + 16)
                    cx, csh, cy = comb(n)
                    b = g * 2 + n
                    sp.dma_start(cx, x_b[bass.ds(b, 1)].rearrange("a p t c -> p (a t) c")).then_inc(c_in[n], 16)
                    sp.dma_start(csh, shared_b[bass.ds(b, 1)].rearrange("a p t c -> p (a t) c")).then_inc(c_in[n], 16)
                    sp.dma_start(cy, routed_b[bass.ds(b, 1)].rearrange("a p t c -> p (a t) c")).then_inc(c_in[n], 16)
            for n in range(2):
                sp.wait_ge(c_out[n], 16 * (B // 2 + 1))

        @block.gpsimd
        def _(pool):
            pool.sem_inc(part_added, 2)
            pool.sem_inc(rows_done, 1)
            pool.wait_ge(small_in, 80)

            def low(n):
                src, hi, lo = chunks[n]
                pool.wait_ge(hi_made, n + 1)
                if lo is None:
                    pool.wait_ge(lo_made, n)
                    pool.sem_inc(lo_made, 1)
                else:
                    pool.tensor_tensor(lo, staged(n, hi), hi.bitcast(F32), ALU.subtract).then_inc(lo_made, 1)

            for n in range(EARLY):
                low(n)
            with pool.Fori(0, B) as b:
                pool.wait_ge(mv_done, b * TT + TT)
                pool.sem_inc(pool_turn, 1)
                pool.tensor_scalar(rstd[:, 0, :], mv[:, :, 1], EPS, None, ALU.add).then_inc(pool_ve, 1)
                pool.wait_ge(pool_ve, b + 1)
                pool.tensor_tensor(rstd[:, 1, :], rstd[:, 0, :], k("minus_half"), ALU.pow).then_inc(rstd_done, 1)
                pool.wait_ge(xr_done, b * TT + TT)
                pool.sem_inc(pool_turn, 1)
                pool.tensor_copy(rows[:, bass.ds(b * TT, TT), 0:C], xr).then_inc(rows_done, 1)
            for n in range(EARLY, NCH):
                low(n)
            pool.wait_ge(rows_done, B + 1)
            pool.memset(zpad[:], 0.0).then_inc(pad_done, 1)
            pool.wait_ge(pad_done, 1)
            pool.memset(zpad[:, C:C + 1], FAR).then_inc(pad_done, 1)
            pool.wait_ge(route_done, 1)
            for t in range(NT):
                for j in range(2):
                    pool.indirect_dma_start(
                        slots_dram, bass.IndirectOffsetOnAxis(ap=where[:, j, t:t + 1], axis=0),
                        rows[:, t, :], None, bounds_check=SLOTS - 1, oob_is_err=False).then_inc(scattered, 16)
            pool.wait_ge(pad_done, 2)
            for n in range(E + TAIL):
                pool.indirect_dma_start(
                    slots_dram, bass.IndirectOffsetOnAxis(ap=where_pad[:, n:n + 1], axis=0),
                    zpad, None, bounds_check=SLOTS - 1, oob_is_err=False)\
                    .then_inc(y_out[n % 2] if n < 4 else scattered, 16)

            def batch(b, routed):
                m0 = (b - BLIND) * TILES_B
                for kind, i in batch_plan(routed):
                    if kind == "turn":
                        pool.wait_ge(p_h, b * 2 + i + 1)
                        pool.tensor_tensor(phl[:, :, :, 1, :], prb[:], phl[:, :, :, 0, :].bitcast(F32),
                                           ALU.subtract).then_inc(p_l, 1)
                    if kind == "pv" and i % ND:
                        h, d = i // ND, i % ND
                        n = h * (ND - 1) + d - 1
                        lo = DIST[d]
                        if d == 1:
                            drained(pool, None, b, use_of("pv", i - 1))
                        pool.wait_ge(part_added, b * 18 + n + 2)
                        drained(pool, None, b, use_of("pv", i))
                        pool.tensor_tensor(acc[:, h, lo:T], acc[:, h, lo:T], part[:, n % 2, lo:T],
                                           ALU.add).then_inc(part_added, 1)
                    if kind == "tx":
                        m = m0 + i
                        pool.wait_ge(down_done, m + 1)
                        pool.sem_inc(pool_turn, 1)
                        pool.tensor_copy(pick[:, i % 4, :], tile_row[:, bass.ds(m, 1)].to_broadcast([16, P]))\
                            .then_inc(pick_done, 1)
                    if kind == "down":
                        m = m0 + i
                        pool.wait_ge(home_done, m + 3)
                        pool.wait_ge(y_made, m + 2)
                        pool.sem_inc(pool_turn, 1)
                        pool.indirect_dma_start(
                            routed_dram, bass.IndirectOffsetOnAxis(ap=home[:, i % 4:i % 4 + 1], axis=0),
                            ys[:, i % 2, :], None, bounds_check=2 * NT * P - 1, oob_is_err=False)\
                            .then_inc(y_out[i % 2], 16)

            with pool.Fori(0, BLIND) as b:
                batch(b, False)
            with pool.Fori(BLIND, B) as b:
                batch(b, True)
            with pool.Fori(0, B // 2) as g:
                for n in range(2):
                    b = g * 2 + n
                    cx, csh, cy = comb(n)
                    pool.wait_ge(silu_done, b + 1)
                    pool.tensor_tensor(cy[:, :, 0:C], csh, xnt[:, bass.ds(b, 1), :].rearrange("p a (t c) -> p (a t) c", c=C),
                                       ALU.mult).then_inc(sg_done, 1)

        @block.scalar
        def _(act):
            def wait(s, v):
                hold(act, act_turn, s, v)

            act.sem_inc(sh_stored, 16)
            act.sem_inc(xt_done, 1)
            act.sem_inc(gelu_done, 1)
            act.sem_inc(y_made, 1)

            def high(n):
                src, hi, lo = chunks[n]
                act.wait_ge(raw_in[n % RING], 16 * (n // RING + 1))
                act.activation(hi, staged(n, hi), ACT.Copy).then_inc(hi_made, 1)

            for n in range(EARLY):
                high(n)
            with act.Fori(0, B) as b:
                for c in range(CH):
                    wait(t_done, b * CH + c + 1)
                    wait(logit_done, b + 1)
                    act.activation(xt_f[:, c, :], bank_d[c][:], ACT.Copy).then_inc(xt_done, 1)
                    act.activation(xnt[:, bass.ds(b, 1), c * T:(c + 1) * T].rearrange("p a n -> p (a n)"),
                                   bank_d[c][:], ACT.Copy).then_inc(xt_done, 1)
            for n in range(EARLY, NCH):
                high(n)
            act.wait_ge(gap_done, 1)
            act.activation(weight[:, 1, :], rk[7][:, 0:NT], ACT.Exp).then_inc(exp_done, 1)

            def batch(b, routed):
                def full(use):
                    wait(d_full[use % BANKS], b * BANK_USES + use // BANKS + 1)
                    return bank_d[use % BANKS], d_free[use % BANKS]

                m0 = (b - BLIND) * TILES_B
                for kind, i in batch_plan(routed):
                    if kind == "split":
                        act.activation(t_h[:].rearrange("p c n -> p (c n)"),
                                       xnt[:, bass.ds(b, 1), :].rearrange("p a n -> p (a n)"), ACT.Copy).then_inc(split_h, 1)
                    if kind == "qkv":
                        half, which = divmod(i, 3)
                        src, free = full(USE[kind, i][0])
                        act.activation(qkv[:, i, :], src[:], ACT.Identity,
                                       bias=bqkv[:, which * CH + half:which * CH + half + 1]).then_inc(free, 1)
                    if kind == "shared_up":
                        src, free = full(USE[kind, i][0])
                        wait(sh_stored, b * 16 + 16)
                        act.activation(hs[:, i, :], src[:], ACT.Gelu, bias=bs1[:, i:i + 1]).then_inc(free, 1)
                        if i == 1:
                            for j in range(2):
                                drained(act, act_turn, b, use_of(kind, j))
                            act.activation(t_h[:], hs[:], ACT.Copy).then_inc(hs_h, 1)
                    if kind == "shared_down":
                        src, free = full(USE[kind, i][0])
                        wait(hs_l, b + 1)
                        act.activation(sh_out[:, 2 * i:2 * i + 2, :].rearrange("p t c -> p (t c)"), src[:], ACT.Copy)\
                            .then_inc(free, 1)
                    if kind == "soft_norm":
                        wait(shifted, b * 2 + i + 1)
                        act.activation(prb[:], sco[:], ACT.Exp, scale=SCALE).then_inc(exped, 1)
                    if kind == "turn":
                        wait(normed, b * 2 + i + 1)
                        act.activation(phl[:, :, :, 0, :], prb[:], ACT.Copy).then_inc(p_h, 1)
                        for j, use in enumerate(USE[kind, i]):
                            src, free = full(use)
                            act.activation(turned[:, i, j, :], src[:], ACT.Copy).then_inc(free, 1)
                    if kind == "mix_split":
                        wait(part_added, b * 18 + 20)
                        act.activation(t_h[:], acc[:], ACT.Copy).then_inc(mix_h, 1)
                    if kind == "project":
                        src, free = full(USE[kind, i][0])
                        act.activation(xnt[:, bass.ds(b, 1), i * T:(i + 1) * T].rearrange("p a n -> p (a n)"),
                                       src[:], ACT.Copy).then_inc(free, 1)
                    m = m0 + i
                    if kind == "tx":
                        wait(tx_done, m + 3)
                        wait(up_done, m + 1)
                        act.activation(xs_h[:].rearrange("p c n -> p (c n)"), bank_tx[:, 0:C], ACT.Copy).then_inc(xs_hi, 1)
                    if kind == "up":
                        wait(up_done, m + 2)
                        wait(th_done, m + 1)
                        act.activation(hr[:], bank_up[:, 0:C], ACT.Gelu).then_inc(gelu_done, 1)
                    if kind == "th":
                        wait(th_done, m + 2)
                        wait(down_done, m + 4)
                        act.activation(hr_h[:].rearrange("p c n -> p (c n)"), bank_th[:, 0:C], ACT.Copy).then_inc(hr_hi, 1)
                    if kind == "down":
                        wait(down_done, m + 5)
                        wait(y_out[i % 2], 16 * ((b - BLIND) * (TILES_B // 2) + i // 2 + 2))
                        act.activation(ys[:, i % 2, :], bank_down[:, 0:C], ACT.Copy).then_inc(y_made, 1)

            with act.Fori(0, BLIND) as b:
                batch(b, False)
            with act.Fori(BLIND, B) as b:
                batch(b, True)

            act.sem_inc(c_out[0], 16)
            act.sem_inc(c_out[1], 16)
            with act.Fori(0, B // 2) as g:
                for n in range(2):
                    b = g * 2 + n
                    cx, csh, cy = comb(n)
                    wait(g_parts, b * 8 + 8)
                    act.activation(csh, cy[:, :, C:2 * C], ACT.Silu).then_inc(silu_done, 1)
                    wait(o_made, b + 1)
                    act.dma_start(out_b[bass.ds(b, 1)].rearrange("a p t c -> p (a t) c"), cx).then_inc(c_out[n], 16)

        @block.vector
        def _(dve):
            count = [0]

            def step(ins, base=None):
                count[0] += 1
                ins.then_inc(dve_done, 1)
                dve.wait_ge(dve_done, count[0] if base is None else base + count[0])

            dve.sem_inc(s_free, 1)
            dve.sem_inc(lg_done, 1)
            dve.wait_ge(small_in, 80)
            dve.wait_ge(brow_in, 32)
            for j, raw in enumerate((sco, prb)):
                r = raw[0:16].rearrange("p a b c -> p (a b c)")[:, 0:C]
                dst = brow[:, j * C:(j + 1) * C]
                tmp = part[0:16, 0, j * C:(j + 1) * C]
                step(dve.tensor_copy(dst, r))
                step(dve.tensor_tensor(tmp, r, dst.bitcast(F32), ALU.subtract))
                step(dve.tensor_scalar(tmp, tmp, k("row_lo")[0:16], None, ALU.mult))
                step(dve.scalar_tensor_tensor(dst, dst.bitcast(F32), k("row_hi")[0:16], tmp, ALU.mult, ALU.add))
            step(dve.tensor_scalar(part[0:16, 1, 0:P], k("ones")[0:16], k("row_expert")[0:16], None, ALU.mult))
            step(dve.tensor_scalar(dense_pick[:], part[0:16, 1, 0:P], -1.0, None, ALU.is_equal))
            before = count[0]

            for b in range(B):
                dve.wait_ge(x_in[b], 16)
            with dve.Fori(0, B) as b:
                count[0] = 0
                for t in range(TT):
                    at = rows[:, bass.ds(b * TT + t, 1), 0:C].rearrange("p a n -> p (a n)")
                    dve.bn_stats(stats[:, t, :], at).then_inc(dve_done, 1)
                hold(dve, dve_turn, dve_done, b * TT + (before + TT))
                for t in range(TT):
                    dve.bn_aggr(mv[:, t, :], stats[:, t, :]).then_inc(mv_done, 1)
                dve.wait_ge(mv_done, b * TT + TT)
                dve.wait_ge(rstd_done, b + 1)
                dve.wait_ge(rows_done, b + 1)
                for t in range(TT):
                    at = rows[:, bass.ds(b * TT + t, 1), 0:C].rearrange("p a n -> p (a n)")
                    dve.tensor_scalar(xr[:, t, :], at, mv[:, t, 0:1], rstd[:, 1, t:t + 1], ALU.subtract, ALU.mult)\
                        .then_inc(xr_done, 1)
                dve.wait_ge(logit_done, b + 2)
                dve.tensor_tensor(lg[:, bass.ds(b * TT, TT), :],
                                  bank_s[:, 0:TT * 8].rearrange("p (t e) -> p t e", e=8)[:, :, 0:E],
                                  ebias[:].rearrange("p (a e) -> p a e", a=1).to_broadcast([P, TT, E]), ALU.add)\
                    .then_inc(lg_done, 1)
            count[0] = before + B * TT
            dve.wait_ge(lg_done, B + 1)
            dve.wait_ge(rows_done, B + 1)

            def te(a):
                return a[:, 0:NT * E].rearrange("p (t e) -> p t e", e=E)

            def row_e(a):
                return a.rearrange("p (a e) -> p a e", a=1).to_broadcast([P, NT, E])

            rank, win, sel1, sel2, slot, tmp, total = map(te, rk[0:7])
            small = rk[7]
            step(dve.tensor_copy(rank, row_e(k("rank0"))))
            for s in range(1, E):
                step(dve.tensor_tensor(win[:, :, 0:E - s], lg[:, :, 0:E - s], lg[:, :, s:E], ALU.is_ge))
                step(dve.tensor_tensor(rank[:, :, s:E], rank[:, :, s:E], win[:, :, 0:E - s], ALU.add))
                step(dve.tensor_tensor(rank[:, :, 0:E - s], rank[:, :, 0:E - s], win[:, :, 0:E - s], ALU.subtract))
            step(dve.tensor_scalar(sel1, rank, 0.0, None, ALU.is_equal))
            step(dve.tensor_scalar(sel2, rank, 1.0, None, ALU.is_equal))
            dve.tensor_tensor(win, sel1, sel2, ALU.add).then_inc(rank_done, 1)
            dve.wait_ge(rank_done, 1)
            step(dve.tensor_tensor(tmp, sel2, lg, ALU.mult))
            step(dve.tensor_reduce(weight[:, 1, :], tmp, AX.X, ALU.add))
            step(dve.tensor_reduce(weight[:, 0, :], lg, AX.X, ALU.max))
            dve.tensor_tensor(small[:, 0:NT], weight[:, 1, :], weight[:, 0, :], ALU.subtract).then_inc(gap_done, 1)
            step(dve.tensor_tensor(tmp, sel1, row_e(k("expert")), ALU.mult))
            step(dve.tensor_reduce(rows[:, :, C + 1:C + 2].rearrange("p t a -> p (t a)"), tmp, AX.X, ALU.add))
            step(dve.tensor_copy(rows[:, :, C:C + 1].rearrange("p t a -> p (t a)"), k("token2")))
            dve.wait_ge(count_done, 2)
            step(dve.tensor_copy(total, te(bank_tx)))
            for e in range(E):
                step(dve.tensor_tensor_scan(tmp[:, :, e], k("ones")[:, 0:NT], total[:, :, e], 0.0, ALU.mult, ALU.add))
            cnt = small[:, 32:32 + E]
            tiles = small[:, 40:40 + E]
            end = small[:, 48:48 + E]
            base = small[:, 56:56 + E]
            over = small[:, 64:64 + E]
            pad = small[:, 80:80 + E + TAIL]
            step(dve.tensor_copy(cnt, tmp[:, NT - 1, :]))
            step(dve.tensor_tensor(slot, tmp, total, ALU.subtract))
            step(dve.tensor_tensor(slot, slot, te(bank_s), ALU.add))
            et = rk[1][:, 0:E * NT].rearrange("p (e t) -> p e t", t=NT)
            step(dve.tensor_tensor(et, cnt.rearrange("p (e a) -> p e a", a=1).to_broadcast([P, E, NT]),
                                   k("edges").rearrange("p (a t) -> p a t", a=1).to_broadcast([P, E, NT]), ALU.is_gt))
            step(dve.tensor_reduce(tiles, et, AX.X, ALU.add))
            step(dve.tensor_tensor_scan(end, k("ones")[:, 0:E], tiles, 0.0, ALU.mult, ALU.add))
            step(dve.tensor_tensor(base, end, tiles, ALU.subtract))
            step(dve.tensor_scalar(base, base, float(P), None, ALU.mult))
            step(dve.tensor_tensor(slot, slot, row_e(base), ALU.add))
            for j, sel in enumerate((sel1, sel2)):
                step(dve.tensor_tensor(tmp, sel, slot, ALU.mult))
                step(dve.tensor_reduce(rk[1][:, j * NT:(j + 1) * NT], tmp, AX.X, ALU.add))
                step(dve.tensor_copy(where[:, j, :], rk[1][:, j * NT:(j + 1) * NT]))
            je = qf[:, 0:RT * E].rearrange("p (j e) -> p j e", e=E)
            step(dve.tensor_tensor(je, k("tile_no").rearrange("p (j a) -> p j a", a=1).to_broadcast([P, RT, E]),
                                   end.rearrange("p (a e) -> p a e", a=1).to_broadcast([P, RT, E]), ALU.is_ge))
            step(dve.tensor_reduce(tile_ef[:], je, AX.X, ALU.add))
            step(dve.tensor_scalar(tile_ef[:], tile_ef[:], float(E - 1), None, ALU.min))
            step(dve.tensor_copy(tile_ei[:], tile_ef[0:1, :]))
            step(dve.tensor_scalar(tile_row[:], tile_ef[0:16, :], k("row_expert")[0:16], None, ALU.is_equal))
            step(dve.tensor_scalar(end, end, float(P), None, ALU.mult))
            step(dve.tensor_tensor(pad[:, 0:E], base, cnt, ALU.add))
            step(dve.tensor_scalar(pad[:, 0:E], pad[:, 0:E], k("lane"), None, ALU.add))
            step(dve.tensor_tensor(over, pad[:, 0:E], end, ALU.is_ge))
            step(dve.scalar_tensor_tensor(pad[:, 0:E], over, FAR, pad[:, 0:E], ALU.mult, ALU.add))
            step(dve.tensor_scalar(pad[:, E:], k("tail"), end[:, E - 1:E], None, ALU.add))
            step(dve.tensor_copy(where_pad[:], pad))
            dve.wait_ge(exp_done, 1)
            step(dve.tensor_scalar(small[:, 0:NT], weight[:, 1, :], 1.0, None, ALU.add))
            step(dve.reciprocal(weight[:, 0, :], small[:, 0:NT]))
            dve.tensor_tensor(weight[:, 1, :], weight[:, 1, :], weight[:, 0, :], ALU.mult).then_inc(route_done, 1)
            dve.wait_ge(route_done, 1)
            dve.wait_ge(lo_made, NCH)
            base_n = count[0]

            def batch(b, routed, per, start):
                count[0] = 0
                origin = b * per + start if not isinstance(b, int) else None

                def mark(ins):
                    step(ins, origin)

                def full(use):
                    dve.wait_ge(d_full[use % BANKS], b * BANK_USES + use // BANKS + 1)
                    return bank_d[use % BANKS], d_free[use % BANKS]

                m0 = (b - BLIND) * TILES_B
                for kind, i in batch_plan(routed):
                    m = m0 + i
                    if kind == "split":
                        dve.wait_ge(split_h, b + 1)
                        dve.tensor_tensor(t_l[:].rearrange("p c n -> p (c n)"),
                                          xnt[:, bass.ds(b, 1), :].rearrange("p a n -> p (a n)"),
                                          t_h[:].rearrange("p c n -> p (c n)").bitcast(F32), ALU.subtract)\
                            .then_inc(split_l, 1)
                    if kind in ("product", "product_rest"):
                        for j in range(2):
                            drained(dve, None, b, use_of("qkv", 3 * i + j))
                        for d in range(ND)[:RING] if kind == "product" else range(ND)[RING:]:
                            lo = DIST[d]
                            n = i * ND + d
                            dve.wait_ge(prod_used, b * 2 * ND + n + 1)
                            dve.tensor_tensor(prod[:, n % RING, lo:T], qkv[:, 3 * i, lo:T], qkv[:, 3 * i + 1, 0:T - lo],
                                              ALU.mult).then_inc(prod_ready, 1)
                    if kind == "soft_max":
                        dve.wait_ge(prod_used, b * 2 * ND + (i + 1) * ND + RING)
                        s4 = bank_s[:, 0:TT * ND * HH].rearrange("p (t d h) -> p t d h", d=ND, h=HH)
                        msk = k("mask").rearrange("p (t d a) -> p t d a", d=ND, a=1).to_broadcast([P, TT, ND, HH])
                        dve.tensor_tensor(sco[:], s4, msk, ALU.add).then_inc(s_free, 1)
                        dve.wait_ge(s_free, b * 2 + i + 2)
                        mark(dve.tensor_reduce(red[:, 0], sco[:].rearrange("p t d h -> p t h d"), AX.X, ALU.max))
                        dve.tensor_tensor(sco[:], sco[:],
                                          red[:, 0:1].rearrange("p a t h -> p t a h").to_broadcast([P, TT, ND, HH]),
                                          ALU.subtract).then_inc(shifted, 1)
                    if kind == "soft_norm":
                        dve.wait_ge(exped, b * 2 + i + 1)
                        mark(dve.tensor_reduce(red[:, 1], prb[:].rearrange("p t d h -> p t h d"), AX.X, ALU.add))
                        mark(dve.reciprocal(red[:, 2], red[:, 1]))
                        dve.tensor_tensor(prb[:], prb[:],
                                          red[:, 2:3].rearrange("p a t h -> p t a h").to_broadcast([P, TT, ND, HH]),
                                          ALU.mult).then_inc(normed, 1)
                    if kind == "shared_up" and i == 1:
                        dve.wait_ge(hs_h, b + 1)
                        dve.tensor_tensor(t_l[:], hs[:], t_h[:].bitcast(F32), ALU.subtract).then_inc(hs_l, 1)
                    if kind == "pv":
                        h, d = i // ND, i % ND
                        lo = DIST[d]
                        src, free = full(USE[kind, i][0])
                        if d == 0:
                            dve.wait_ge(sh_stored, b * 16 + 32)
                            dve.wait_ge(mix_l, b + 1)
                            drained(dve, None, b, use_of("qkv", 3 * h + 2))
                            dve.tensor_tensor(acc[:, h, :], src[:], qkv[:, 3 * h + 2, :], ALU.mult).then_inc(free, 1)
                        else:
                            n = h * (ND - 1) + d - 1
                            dve.wait_ge(part_added, b * 18 + n + 1)
                            at = lo % 2
                            dve.tensor_tensor(part[:, n % 2, lo:T], src[:, at:at + T - lo], qkv[:, 3 * h + 2, 0:T - lo],
                                              ALU.mult).then_inc(free, 1)
                    if kind == "mix_split":
                        dve.wait_ge(mix_h, b + 1)
                        dve.tensor_tensor(t_l[:], acc[:], t_h[:].bitcast(F32), ALU.subtract).then_inc(mix_l, 1)
                    if kind == "tx":
                        dve.wait_ge(xs_in[i % 2], 16 * ((b - BLIND) * (TILES_B // 2) + i // 2 + 1))
                        dve.wait_ge(home_done, m + 2)
                        dve.tensor_tensor(homef[:, 0:1], xs[:, i % 2, C + 1:C + 2], tile_ef[:, bass.ds(m, 1)],
                                          ALU.not_equal).then_inc(home_f, 1)
                        dve.wait_ge(home_f, m + 1)
                        dve.wait_ge(y_out[i % 2], 16 * ((b - BLIND) * (TILES_B // 2) + i // 2 + 1))
                        dve.tensor_tensor(home[:, i % 4:i % 4 + 1], homef[:, 0:1], xs[:, i % 2, C:C + 1],
                                          ALU.add).then_inc(home_done, 1)
                        dve.wait_ge(xs_hi, m + 1)
                        dve.tensor_tensor(xs_l[:].rearrange("p c n -> p (c n)"), bank_tx[:, 0:C],
                                          xs_h[:].rearrange("p c n -> p (c n)").bitcast(F32), ALU.subtract)\
                            .then_inc(xs_lo, 1)
                    if kind == "th":
                        dve.wait_ge(hr_hi, m + 1)
                        dve.tensor_tensor(hr_l[:].rearrange("p c n -> p (c n)"), bank_th[:, 0:C],
                                          hr_h[:].rearrange("p c n -> p (c n)").bitcast(F32), ALU.subtract)\
                            .then_inc(hr_lo, 1)
                return count[0]

            dve.sem_inc(home_done, 2)
            dve.sem_inc(xs_lo, 1)
            dve.sem_inc(hr_lo, 1)
            dve.sem_inc(mix_l, 1)
            per = 2 * 3
            with dve.Fori(0, BLIND) as b:
                assert batch(b, False, per, base_n) == per
            with dve.Fori(BLIND, B) as b:
                assert batch(b, True, per, base_n) == per

            with dve.Fori(0, B // 2) as g:
                for n in range(2):
                    b = g * 2 + n
                    cx, csh, cy = comb(n)
                    dve.wait_ge(c_in[n], g * 48 + 48)
                    for j in range(2):
                        for t in range(TT):
                            w = weight[:, j, bass.ds(b * TT + t, 1)]
                            half = cy[:, t, j * C:(j + 1) * C]
                            other = csh[:, t, :] if j == 0 else cy[:, t, 0:C]
                            ins = dve.scalar_tensor_tensor(half, half, w, other, ALU.mult, ALU.add)
                            ins.then_inc(g_parts, 1)
                        dve.wait_ge(g_parts, b * 8 + j * 4 + 4)
                    dve.wait_ge(sg_done, b + 1)
                    dve.tensor_tensor(cx, cx, cy[:, :, 0:C], ALU.add).then_inc(o_made, 1)

        @block.tensor
        def _(pe):
            for i in range(BANKS):
                pe.sem_inc(d_free[i], 1)
            pe.sem_inc(logit_done, 1)
            pe.sem_inc(prod_used, RING)
            pe.sem_inc(tx_done, 2)
            pe.sem_inc(up_done, 1)
            pe.sem_inc(th_done, 1)
            pe.sem_inc(down_done, 4)
            pe.wait_ge(small_in, 80)
            with pe.Fori(0, B) as b:
                pe.wait_ge(xr_done, b * TT + TT)
                pe.wait_ge(xt_done, b * 2 * CH + 1)
                for c in range(CH):
                    for t in range(TT):
                        last = pe.transpose(bank_d[c][:, t * P:(t + 1) * P], xr[:, t, c * P:(c + 1) * P], ident)
                    last.then_inc(t_done, 1)
                pe.wait_ge(xt_done, b * 2 * CH + 2 * CH + 1)
                pe.wait_ge(lg_done, b + 1)
                for t in range(TT):
                    for c in range(CH):
                        last = pe.matmul(bank_s[:, t * 8:t * 8 + E], xt_f[:, c, t * P:(t + 1) * P], gate[:, c, :],
                                         start=c == 0, stop=c == CH - 1)
                last.then_inc(logit_done, 1)
            pe.wait_ge(rank_done, 1)
            win = rk[1][:, 0:NT * E]
            pe.matmul(bank_s[:, 0:NT * E], k("before"), win, start=True, stop=True).then_inc(count_done, 1)
            pe.matmul(bank_tx[:, 0:NT * E], k("ones"), win, start=True, stop=True).then_inc(count_done, 1)
            pe.wait_ge(route_done, 1)
            pe.wait_ge(lo_made, NCH)

            def three(dst, left, right, first=True, last=True):
                n = 0
                for c in range(CH):
                    for a, w in ((0, 0), (0, 1), (1, 0)):
                        mm = pe.matmul(dst, left[a](c), right[w](c), start=first and n == 0,
                                       stop=last and n == 3 * CH - 1)
                        n += 1
                return mm

            def batch(b, routed):
                def take(use):
                    pe.wait_ge(d_free[use % BANKS], b * BANK_USES + use // BANKS + 1)
                    return bank_d[use % BANKS], d_full[use % BANKS]

                m0 = (b - BLIND) * TILES_B
                experts = [pe.value_load(tile_ei[0:1, bass.ds(m0 + i, 1)], min_val=0, max_val=E - 1)
                           for i in range(TILES_B)] if routed else []
                for kind, i in batch_plan(routed):
                    m = m0 + i
                    if kind == "split":
                        pe.wait_ge(split_l, b + 1)
                    if kind == "qkv":
                        half, which = divmod(i, 3)
                        col = which * C + half * P
                        dst, fullsem = take(USE[kind, i][0])
                        three(dst[:], [lambda c: wqkv_h[:, c, col:col + P], lambda c: wqkv_l[:, c, col:col + P]],
                              [lambda c: t_h[:, c, :], lambda c: t_l[:, c, :]]).then_inc(fullsem, 1)
                    if kind == "shared_up":
                        dst, fullsem = take(USE[kind, i][0])
                        s = slice(i * P, (i + 1) * P)
                        three(dst[:], [lambda c: w1_h[:, SHARED, c, s], lambda c: w1_l[:, SHARED, c, s]],
                              [lambda c: t_h[:, c, :], lambda c: t_l[:, c, :]]).then_inc(fullsem, 1)
                    if kind in ("shared_down", "project"):
                        dst, fullsem = take(USE[kind, i][0])
                        if kind == "project":
                            pe.wait_ge(mix_l, b + 2)
                            wh, wl = (lambda c: wp_h[:, c, :]), (lambda c: wp_l[:, c, :])
                        else:
                            pe.wait_ge(hs_l, b + 1)
                            wh, wl = (lambda c: w2_h[:, SHARED, c, :]), (lambda c: w2_l[:, SHARED, c, :])
                        bias = brow[:, 0:C] if kind == "project" else brow[:, C:2 * C]
                        for j in range(2):
                            s = slice((2 * i + j) * P, (2 * i + j + 1) * P)
                            o = dst[:, j * C:(j + 1) * C]
                            three(o, [lambda c: t_h[:, c, s], lambda c: t_l[:, c, s]], [wh, wl], last=False)
                            mm = pe.matmul(o, dense_pick[:], bias, start=False, stop=True)
                        mm.then_inc(fullsem, 1)
                    if kind == "scores":
                        pe.wait_ge(s_free, b * 2 + i + 1)
                        for d in range(ND):
                            n = i * ND + d
                            pe.wait_ge(prod_ready, b * 2 * ND + n + 1)
                            for t in range(TT):
                                at = (t * ND + d) * HH
                                mm = pe.matmul(bank_s[:, at:at + HH], prod[:, n % RING, t * P:(t + 1) * P],
                                               k("head_sum"), start=True, stop=True)
                            mm.then_inc(prod_used, 1)
                    if kind == "turn":
                        pe.wait_ge(p_l, b * 2 + i + 1)
                        flat = phl[:].rearrange("p t d a h -> p t (d a h)").bitcast(F32)
                        for j, use in enumerate(USE[kind, i]):
                            dst, fullsem = take(use)
                            n0 = (0, SECOND * 2 * HH)[j]
                            for t in range(TT):
                                mm = pe.transpose(dst[:, t * P:(t + 1) * P], flat[:, t, n0:n0 + P], ident)
                            mm.then_inc(fullsem, 1)
                    if kind == "pv":
                        h, d = i // ND, i % ND
                        if d == 0:
                            for j in range(2):
                                drained(pe, None, b, use_of("turn", h, j))
                        dst, fullsem = take(USE[kind, i][0])
                        lo = DIST[d] // 2 * 2
                        j, pick_d = (0, d) if d < 8 else (1, d - SECOND)
                        pe.matmul(dst[:, 0:T - lo], sp_r[:, pick_d, :], turned[:, h, j, lo:T], start=True, stop=True)\
                            .then_inc(fullsem, 1)
                    if kind == "tx":
                        pe.wait_ge(xs_in[i % 2], 16 * ((b - BLIND) * (TILES_B // 2) + i // 2 + 1))
                        pe.wait_ge(xs_lo, m + 1)
                        for c in range(CH):
                            mm = pe.transpose(bank_tx[:, c * P:(c + 1) * P], xs[:, i % 2, c * P:(c + 1) * P], ident)
                        mm.then_inc(tx_done, 1)
                    if kind == "th":
                        pe.wait_ge(gelu_done, m + 2)
                        pe.wait_ge(hr_lo, m + 1)
                        for c in range(CH):
                            mm = pe.transpose(bank_th[:, c * P:(c + 1) * P], hr[:, c * P:(c + 1) * P], ident)
                        mm.then_inc(th_done, 1)
                    if kind in ("up", "down"):
                        up = kind == "up"
                        e = experts[i]
                        l_h, l_l = (xs_h, xs_l) if up else (hr_h, hr_l)
                        r_h, r_l = (w1_h, w1_l) if up else (w2_h, w2_l)
                        o = (bank_up if up else bank_down)[:, 0:C]
                        if up:
                            pe.wait_ge(pick_done, m + 1)
                            pe.wait_ge(xs_lo, m + 2)
                            pe.wait_ge(gelu_done, m + 1)
                        else:
                            pe.wait_ge(hr_lo, m + 2)
                            pe.wait_ge(y_made, m + 1)
                        pe.matmul(o, pick[:, i % 4, :], brow[:, 0:C] if up else brow[:, C:2 * C], start=True, stop=False)

                        def moving(r):
                            return lambda c: r[:, bass.ds(e, 1), c, :].rearrange("p a n -> p (a n)")
                        three(o, [lambda c: l_h[:, c, :], lambda c: l_l[:, c, :]], [moving(r_h), moving(r_l)],
                              first=False).then_inc(up_done if up else down_done, 1)

            with pe.Fori(0, BLIND) as b:
                batch(b, False)
            with pe.Fori(BLIND, B) as b:
                batch(b, True)


def kernel(L0_attn_x, L0_attn_W_qkv, L0_attn_b_qkv, L0_attn_W_proj, L0_attn_b_proj, L0_ffn_gate_w,
           L0_ffn_expert_bias, L0_ffn_sw1, L0_ffn_sb1, L0_ffn_sw2, L0_ffn_sb2, L0_ffn_rw1, L0_ffn_rb1,
           L0_ffn_rw2, L0_ffn_rb2):
    import concourse.bacc as bacc
    from concourse.bass_utils import run_bass_kernel_spmd

    a = {k: np.asarray(v) for k, v in dict(
        x=L0_attn_x, w_qkv=L0_attn_W_qkv, w_proj=L0_attn_W_proj, expert_bias=L0_ffn_expert_bias).items()}
    a["b_qkv"] = np.asarray(L0_attn_b_qkv).reshape(-1, P).T
    a["sb1"] = np.asarray(L0_ffn_sb1).reshape(-1, P).T
    a["gate_t"] = np.asarray(L0_ffn_gate_w).T
    a["w1"] = np.concatenate([np.asarray(L0_ffn_rw1), np.asarray(L0_ffn_sw1)[None]])
    a["w2"] = np.concatenate([np.asarray(L0_ffn_rw2), np.asarray(L0_ffn_sw2)[None]])
    routed = np.concatenate([np.asarray(L0_ffn_rb1), np.asarray(L0_ffn_rb2)], axis=1)
    dense = np.concatenate([np.asarray(L0_attn_b_proj), np.asarray(L0_ffn_sb2)])[None]
    a["bias_rows"] = np.concatenate([routed, routed, dense, dense])
    a["consts"], a["spread"] = constants()

    nc = bacc.Bacc("TRN2", target_bir_lowering=False, num_devices=1, dynamic_dma_scratch_size=8192)
    arrays, args = {}, {}
    for name, v in a.items():
        arrays[f"in_{name}"] = np.ascontiguousarray(v)
        args[name] = nc.dram_tensor(f"in_{name}", v.shape, F32, kind="ExternalInput").ap()
    args["out"] = nc.dram_tensor("out_x", (B, T, C), F32, kind="ExternalOutput").ap()
    args["slots_dram"] = nc.dram_tensor("slots", (SLOTS, ROW), F32, kind="Internal").ap()
    args["routed_dram"] = nc.dram_tensor("routed", (2 * B * T, C), F32, kind="Internal").ap()
    args["shared_dram"] = nc.dram_tensor("shared", (B * T, C), F32, kind="Internal").ap()
    build(nc, **args)
    r = run_bass_kernel_spmd(nc, [arrays], core_ids=[0])
    return r.results[0]["out_x"]
```

```python
import itertools
from contextlib import ExitStack

import numpy as np

import concourse.bass as bass
from concourse import mybir

F32 = mybir.dt.float32
F32R = mybir.dt.float32r
U32 = mybir.dt.uint32
I32 = mybir.dt.int32
ALU = mybir.AluOpType
ACT = mybir.ActivationFunctionType
AX = mybir.AxisListType

P = 128
B, T, C = 8, 512, 256
HEADS = 16
DH = C // HEADS
TT = T // P
NT = B * TT
CH = C // P
HH = HEADS // CH
DIST = [0] + [1 << k for k in range(T.bit_length() - 1)]
ND = len(DIST)
ADDS = CH * (ND - 1)
E = 7
SHARED = E
EPS = 1e-5
SCALE = DH ** -0.5
ROW = C + 2
BLIND = 2
TILES_B = 12
RT = (B - BLIND) * TILES_B
SLOTS = RT * P
TAIL = SLOTS // P - 2 * NT
FAR = 1.0e6
SECOND = ND - 8
SENDS = {"qkv": 2, "score": 1, "pv": 1}
RING = 3
PACK = 6
STAGES = 4
SETS = 4
assert RT >= 2 * NT + E - 1

CONST = {}
_at = 0
for _name, _n in (("ident", P), ("head_sum", 2 * (ND - 1) * HH + HH), ("mask", TT * ND), ("before", P), ("ones", P),
                  ("edges", NT), ("tile_no", RT), ("lane", 1), ("rank0", E), ("expert", E),
                  ("token2", NT), ("row_expert", 1), ("row_hi", 1), ("row_lo", 1), ("tail", TAIL), ("octal", PACK),
                  ("minus_half", NT)):
    CONST[_name] = (_at, _n)
    _at += _n
NCONST = _at


def constants():
    c = np.zeros((P, NCONST), np.float32)
    p = np.arange(P)

    def put(name, v):
        at, n = CONST[name]
        c[:, at:at + n] = np.broadcast_to(np.asarray(v, np.float32), (P, n))

    put("ident", np.eye(P))
    put("head_sum", (p[:, None] // DH == np.arange(2 * (ND - 1) * HH + HH)[None, :] - (ND - 1) * HH))
    tok = np.arange(TT)[None, :, None] * P + p[:, None, None]
    put("mask", np.where(tok >= np.array(DIST)[None, None, :], 0.0, -1e30).reshape(P, -1))
    put("before", p[:, None] < p[None, :])
    put("ones", np.ones((1, P)))
    put("edges", np.arange(NT)[None] * P)
    put("tile_no", np.arange(RT)[None])
    put("lane", p[:, None])
    put("rank0", (E - 1 - np.arange(E))[None])
    put("expert", np.arange(E)[None])
    put("token2", 2 * (np.arange(NT)[None] * P + p[:, None]))
    put("row_expert", np.where(p < 2 * E, p % E, -1)[:, None])
    put("row_hi", ((p < E) | (p == 2 * E))[:, None])
    put("row_lo", (((p >= E) & (p < 2 * E)) | (p == 2 * E + 1))[:, None])
    put("tail", np.arange(TAIL)[None] * P + p[:, None])
    put("octal", 8.0 ** np.arange(PACK)[None])
    put("minus_half", np.full((1, NT), -0.5))
    s = np.zeros((8, 2, HH, 8, P), np.float32)
    for d in range(8):
        for ch in range(P):
            s[d, :, ch // DH, d, ch] = 1.0
    return c, s.reshape(P, 8 * P)


def body_plan(own=True, before=True, routed=True):
    plan, tiles = [], []
    for i in range(TILES_B + 3 if routed else 0):
        tiles += [("down", i - 3)] if 0 <= i - 3 < TILES_B else []
        tiles += [("th", i - 2)] if 0 <= i - 2 < TILES_B else []
        tiles += [("up", i - 1)] if 0 <= i - 1 < TILES_B else []
        tiles += [("tx", i)] if i < TILES_B else []

    def mine(kind, *numbers):
        if own:
            plan.extend((kind, i) for i in numbers or (0,))

    def last(kind, *numbers):
        if before:
            plan.extend((kind, i) for i in numbers or (0,))

    def fill(n):
        plan.extend(tiles[:n])
        del tiles[:n]

    mine("split")
    last("pv", ND, ND + 1)
    fill(1)
    last("pv", ND + 2, ND + 3)
    fill(1)
    mine("shared_up", 0)
    last("pv", ND + 4)
    fill(1)
    mine("shared_up", 1)
    fill(1)
    for d in range(5):
        mine("qkv", d)
        last("pv", ND + 5 + d)
        fill(1)
    mine("qkv", 5)
    if not before:
        mine("route")
    mine("product", 0)
    fill(2)
    mine("hs_split")
    mine("score", 0)
    mine("product", 1, 2)
    mine("v_move")
    fill(1)
    for d in range(1, ND):
        mine("score", d)
        if d + 2 < ND:
            mine("product", d + 2)
        if d == 4:
            mine("shared_down", 0, 1)
            last("mix_split")
        if d in (1, 3, 5, 6, 8):
            fill(1)
    last("project", 0)
    fill(1)
    mine("score_turn", 0)
    last("project", 1)
    mine("product", ND, ND + 1)
    mine("soft_max", 0)
    fill(4)
    mine("soft_norm", 0)
    fill(4)
    mine("turn", 0)
    for d in range(ND):
        mine("score", ND + d)
        if d + 2 < ND:
            mine("product", ND + d + 2)
        mine("pv", d)
        fill(1)
    mine("score_turn", 1)
    mine("soft_max", 1)
    fill(5)
    mine("soft_norm", 1)
    fill(5)
    mine("turn", 1)
    fill(len(tiles))
    return plan


def bank_uses(plan):
    takes = dict(turn=2, qkv=1, shared_up=1, shared_down=1, pv=1, project=1)
    use, n = {}, 0
    for stage in plan:
        use[stage] = [n + j for j in range(takes.get(stage[0], 0))]
        n += len(use[stage])
    return use, n // BANKS


BANKS = 3
PLAN_FIRST = body_plan(before=False, routed=False)
PLAN_BLIND = body_plan(routed=False)
PLAN_ROUTED = body_plan()
PLAN_LAST = body_plan(own=False, routed=False)
USE_FIRST, BANK_FIRST = bank_uses(PLAN_FIRST)
USE_MIDDLE, BANK_MIDDLE = bank_uses(PLAN_ROUTED)
USE_LAST, _ = bank_uses(PLAN_LAST)
assert all(sum(map(len, u.values())) % BANKS == 0 for u in (USE_FIRST, USE_MIDDLE))


def plan_of(b, routed):
    return PLAN_ROUTED if routed else (PLAN_FIRST if b == 0 else PLAN_LAST if b == B else PLAN_BLIND)


def bank_use(b, kind, i, j=0):
    first, end = isinstance(b, int) and b == 0, isinstance(b, int) and b == B
    n = (USE_FIRST if first else USE_LAST if end else USE_MIDDLE)[kind, i][j]
    return n % BANKS, n // BANKS if first else b * BANK_MIDDLE + (BANK_FIRST - BANK_MIDDLE + n // BANKS)


def build(nc, x, w_qkv, b_qkv, w_proj, bias_rows, gate_t, expert_bias, w1, w2, sb1, consts, spread,
          out, slots_dram, routed_dram, shared_dram):
    x_b = x.rearrange("b (t p) c -> b p t c", p=P)
    out_b = out.rearrange("b (t p) c -> b p t c", p=P)
    shared_b = shared_dram.rearrange("(b t p) c -> b p t c", p=P, t=TT)
    routed_b = routed_dram.rearrange("(b t p k) c -> b p t (k c)", p=P, t=TT, k=2)
    slots_t = slots_dram.rearrange("(j p) c -> j p c", p=P)

    with ExitStack() as ctx:
        def sb(name, shape, dt=F32):
            return ctx.enter_context(nc.sbuf_tensor(name, shape, dt))

        def bank(name):
            return ctx.enter_context(nc.psum_tensor(name, [P, 512], F32))

        def sem(name):
            return ctx.enter_context(nc.semaphore(name))

        rows = sb("rows", [P, NT, ROW])
        xnt = sb("xnt", [P, B, CH * T])
        wqkv_h, wqkv_l = sb("wqkv_h", [P, CH, 3 * C], F32R), sb("wqkv_l", [P, CH, 3 * C], F32R)
        wp_h, wp_l = sb("wp_h", [P, CH, C], F32R), sb("wp_l", [P, CH, C], F32R)
        sp_r = sb("sp_r", [P, 8, P], F32R)
        cst = sb("cst", [P, NCONST])
        bqkv = sb("bqkv", [P, 6])
        bs1 = sb("bs1", [P, CH])
        gate = sb("gate", [P, CH, E])
        ebias = sb("ebias", [P, E])
        brow = sb("brow", [16, 2 * C], F32R)
        dense_pick = sb("dense_pick", [16, P], F32R)
        t_h, t_l = sb("t_h", [P, CH, T], F32R), sb("t_l", [P, CH, T], F32R)
        qkv = sb("qkv", [P, 7, T])
        prod = sb("prod", [P, RING, T])
        part = sb("part", [P, 2, T])
        acc = sb("acc", [P, CH, T])
        sco = sb("sco", [P, TT, ND, HH])
        prb = sb("prb", [P, TT, ND, HH])
        phl = sb("phl", [P, TT, ND, 2, HH], F32R)
        hs = prod[:, 0:CH, :]
        score_t = prod[:, 2, :]
        red = sb("red", [P, 3, TT, HH])
        turned = sb("turned", [P, CH, 2, T], F32R)
        tile_in = sb("tile_in", [P, 2 * ROW + C])
        xs = tile_in[:, 0:2 * ROW].rearrange("p (a n) -> p a n", a=2)
        hr = tile_in[:, 2 * ROW:2 * ROW + C]
        xs_h, xs_l = sb("xs_h", [P, CH, P], F32R), sb("xs_l", [P, CH, P], F32R)
        hr_h, hr_l = sb("hr_h", [P, CH, P], F32R), sb("hr_l", [P, CH, P], F32R)
        ys = sb("ys", [P, 2, C])
        pick = sb("pick", [16, 4, P], F32R)
        home = sb("home", [P, 4], U32)
        homef = sb("homef", [P, 2])
        lg = part[:].rearrange("p a b -> p (a b)")[:, 0:NT * E].rearrange("p (t e) -> p t e", e=E)
        weight = sb("weight", [P, 2, NT])
        where = sb("where", [P, 2, NT], U32)
        where_pad = sb("where_pad", [P, E + TAIL], U32)
        tile_ef = sb("tile_ef", [P, RT])
        tile_ei = sb("tile_ei", [1, RT // PACK], I32)
        tile_row = sb("tile_row", [16, RT])
        ysf = ys[:].rearrange("p a b -> p (a b)")
        mv = ysf[:, 0:2 * NT].rearrange("p (t a) -> p t a", a=2)
        rstd = ysf[:, 2 * NT:4 * NT].rearrange("p (a t) -> p a t", a=2)
        stats = ysf[:, 4 * NT:4 * NT + 6 * TT].rearrange("p (t a) -> p t a", a=6)

        with ExitStack() as place:
            w1_h, w1_l, w2_h, w2_l = (
                place.enter_context(nc.sbuf_tensor(name, [P, E + 1, CH, C], F32R))
                for name in ("w1_h", "w1_l", "w2_h", "w2_l"))
        comb_in = sb("comb_in", [P, SETS, 3, TT, C])

        def k(name):
            at, n = CONST[name]
            return cst[:, at:at + n]

        ident = k("ident")
        accf, ysf = acc[:].rearrange("p a b -> p (a b)"), ys[:].rearrange("p a b -> p (a b)")
        rk = [f[:, i * 256:(i + 1) * 256] for f, n in ((accf, 4), (part[:, 1, :], 2), (ysf, 2)) for i in range(n)]
        
        xt_f = [qkv[:, 0:CH, :], qkv[:, CH:2 * CH, :]]
        acc_rows = acc[:].rearrange("p c (t n) -> p (c t) n", n=C)
        xr = [acc_rows, qkv[:, 4:6, :].rearrange("p c (t n) -> p (c t) n", n=C)]
        sh_blind = [ys[:].rearrange("p a b -> p (a b)"), tile_in[:, ROW:ROW + 2 * C]]
        rows_f = rows[:].rearrange("p a b -> p (a b)")

        def shared_at(b, at, n):
            return rows_f[:, bass.ds(b * CH * T + at, n)]
        zpad = xs[:, 0, :]

        bank_d = [bank(f"bank_d{i}") for i in range(BANKS)]
        bank_s, bank_tx, bank_up, bank_th, bank_down = map(
            bank, ("bank_s", "bank_tx", "bank_up", "bank_th", "bank_down"))
        xt_bank = [bank_d[0:2], [bank_d[2], bank_th]]
        logit_bank = [bank_s, bank_up]

        x_in = [sem(f"x_in{i}") for i in range(B)]
        small_in = sem("small_in")
        raw_in = [sem(f"raw_in{i}") for i in range(STAGES)]
        hi_made, lo_early, lo_late = sem("hi_made"), sem("lo_early"), sem("lo_late")
        mv_done, rstd_done, pool_ve = sem("mv_done"), sem("rstd_done"), sem("pool_ve")
        xr_done, rows_done = sem("xr_done"), sem("rows_done")
        t_done, xt_done = sem("t_done"), sem("xt_done")
        logit_done, lg_done = sem("logit_done"), sem("lg_done")
        brow_done, brow_in = sem("brow_done"), sem("brow_in")
        rank_done, count_done, gap_done, exp_done = map(sem, ("rank_done", "count_done", "gap_done", "exp_done"))
        route_steps, route_done, pad_done = sem("route_steps"), sem("route_done"), sem("pad_done")
        scattered = sem("scattered")
        d_full = [sem(f"d_full{i}") for i in range(BANKS)]
        d_free = [sem(f"d_free{i}") for i in range(BANKS)]
        split_h, split_l = sem("split_h"), sem("split_l")
        prod_ready, prod_used = sem("prod_ready"), sem("prod_used")
        s_free, sums_out, s_full = map(sem, ("s_free", "sums_out", "s_full"))
        shifted, exped, normed, p_h, p_l = map(sem, ("shifted", "exped", "normed", "p_h", "p_l"))
        part_added = sem("part_added")
        mix_h, mix_l = sem("mix_h"), sem("mix_l")
        hs_h, hs_l, v_moved = sem("hs_h"), sem("hs_l"), sem("v_moved")
        sh_stored, sh_back = [sem("sh_stored0"), sem("sh_stored1")], sem("sh_back")
        xs_in = [sem("xs_in0"), sem("xs_in1")]
        tx_done, xs_hi, xs_lo = sem("tx_done"), sem("xs_hi"), sem("xs_lo")
        up_done, gelu_done = sem("up_done"), sem("gelu_done")
        th_done, hr_hi, hr_lo = sem("th_done"), sem("hr_hi"), sem("hr_lo")
        down_done, y_made = sem("down_done"), sem("y_made")
        y_out = [sem("y_out0"), sem("y_out1")]
        home_f, home_done, pick_done = sem("home_f"), sem("home_done"), sem("pick_done")
        dve_done = sem("dve_done")
        act_turn, pool_turn, dve_turn, sp_turn = map(sem, ("act_turn", "pool_turn", "dve_turn", "sp_turn"))
        c_in = [sem(f"c_in{i}") for i in range(SETS)]
        g_parts, silu_done, sg_done, o_made = sem("g_parts"), sem("silu_done"), sem("sg_done"), sem("o_made")
        c_out = [sem(f"c_out{i}") for i in range(SETS)]

        stage = [prod[:, i, :] for i in range(RING)] + [part[:, 1, :]]
        wq = w_qkv.rearrange("(c p) n -> p c n", p=P)
        dense_chunks = [(wq[:, :, h * C:(h + 1) * C], wqkv_h[:, :, h * C:(h + 1) * C], wqkv_l[:, :, h * C:(h + 1) * C])
                        for h in range(3)]
        dense_chunks += [(w_proj.rearrange("(c p) n -> p c n", p=P), wp_h[:], wp_l[:])]
        LOOPED = 2 * (E + 1)
        LOWS = STAGES + LOOPED

        def expert_chunk(g, j):
            e = bass.ds(g * 2 + j // 2, 1)
            raw, hi, lo = (w1, w1_h, w1_l) if j % 2 == 0 else (w2, w2_h, w2_l)
            return (raw[e].rearrange("a (c p) n -> p (a c) n", p=P),
                    hi[:, e].rearrange("p a c n -> p (a c) n"), lo[:, e].rearrange("p a c n -> p (a c) n"))

        def spread_chunk(j):
            return spread[:, j * 512:(j + 1) * 512], sp_r[:, 4 * j:4 * j + 4, :]

        def product_at(i):
            return prod[:, (i + 2) % RING, :]

        def staged(j, like):
            return stage[j].rearrange("p (c n) -> p c n", c=like.shape[1])

        def hold(eng, turn, s, v):
            eng.wait_ge(s, v)
            if turn is not None and not isinstance(v, int):
                eng.sem_inc(turn, 1)

        def drained(eng, turn, b, kind, i, j=0):
            k, n = bank_use(b, kind, i, j)
            hold(eng, turn, d_free[k], n + 2)

        def comb(n):
            co = qkv[:, 2 * n:2 * n + 2, :] if n < 3 else prod[:, 0:2, :]
            return (comb_in[:, n, 0], comb_in[:, n, 1:3].rearrange("p a t c -> p (a t c)").rearrange("p (t c) -> p t c", t=TT),
                    co.rearrange("p a (t c) -> p (a t) c", c=C))

        block = ctx.enter_context(nc.Block())

        @block.sync
        def _(sp):
            for b in range(2):
                sp.dma_start(rows[:, b * TT:(b + 1) * TT, 0:C], x_b[b]).then_inc(x_in[b], 16)
            sp.dma_start(cst[:], consts).then_inc(small_in, 16)
            sp.dma_start(bqkv[:], b_qkv).then_inc(small_in, 16)
            sp.dma_start(bs1[:], sb1).then_inc(small_in, 16)
            sp.dma_start(gate[:], gate_t.rearrange("(c p) e -> p c e", p=P)).then_inc(small_in, 16)
            sp.dma_start(ebias[:], expert_bias.rearrange("(a e) -> a e", a=1).to_broadcast([P, E])).then_inc(small_in, 16)
            sp.dma_start(sco[0:16].rearrange("p a b c -> p (a b c)")[:, 0:256], bias_rows[:, 0:C]).then_inc(brow_in, 16)
            sp.dma_start(prb[0:16].rearrange("p a b c -> p (a b c)")[:, 0:256], bias_rows[:, C:2 * C]).then_inc(brow_in, 16)
            for b in range(2, B):
                sp.dma_start(rows[:, b * TT:(b + 1) * TT, 0:C], x_b[b]).then_inc(x_in[b], 16)
            for j, (src, hi, lo) in enumerate(dense_chunks):
                sp.dma_start(staged(j, src), src).then_inc(raw_in[j], 16)
            sp.wait_ge(lo_early, STAGES)
            with sp.Fori(0, LOOPED // STAGES) as g:
                for j in range(STAGES):
                    hold(sp, sp_turn, lo_late, g * STAGES + j + 1)
                    src, hi, lo = expert_chunk(g, j)
                    sp.dma_start(staged(j, src), src).then_inc(raw_in[j], 16)
            for j in range(2):
                sp.wait_ge(lo_late, LOOPED + j + 1)
                sp.dma_start(stage[j], spread_chunk(j)[0]).then_inc(raw_in[j], 16)

            for b in range(BLIND):
                for i in range(2):
                    drained(sp, None, b, "shared_down", i)
                    sp.dma_start(shared_b[b, :, 2 * i:2 * i + 2, :], sh_blind[i].rearrange("p (t c) -> p t c", c=C))\
                        .then_inc(sh_stored[i], 16)
            sp.wait_ge(scattered, 16 * (2 * NT + E + TAIL - 4))
            for n in range(2):
                sp.wait_ge(y_out[n], 32)
            for n in range(2):
                sp.wait_ge(sh_stored[n], 16 * BLIND)

            def tile_in(m, i):
                hold(sp, sp_turn, tx_done, m + 1)
                hold(sp, sp_turn, home_done, m + 1)
                sp.dma_start(xs[:, i % 2, :], slots_t[bass.ds(m, 1)].rearrange("a p c -> p (a c)"))\
                    .then_inc(xs_in[i % 2], 16)

            with sp.Fori(BLIND, B) as b:
                for kind, i in PLAN_ROUTED:
                    if kind == "tx":
                        tile_in((b - BLIND) * TILES_B + i, i)
            for b in range(BLIND):
                sp.dma_start(rows_f[:, b * CH * T:(b + 1) * CH * T].rearrange("p (t c) -> p t c", c=C), shared_b[b])\
                    .then_inc(sh_back, 16)

            for n in range(2):
                sp.wait_ge(y_out[n], 16 * (RT // 2 + 2))
            with sp.Fori(0, B // SETS) as g:
                for n in range(SETS):
                    hold(sp, sp_turn, c_out[n], g * 16 + 16)
                    cx, cy, co = comb(n)
                    b = g * SETS + n
                    sp.dma_start(cy, routed_b[bass.ds(b, 1)].rearrange("a p t c -> p (a t) c")).then_inc(c_in[n], 16)
                    sp.dma_start(cx, x_b[bass.ds(b, 1)].rearrange("a p t c -> p (a t) c")).then_inc(c_in[n], 16)
            for n in range(SETS):
                sp.wait_ge(c_out[n], 16 * (B // SETS + 1))

        @block.gpsimd
        def _(pool):
            pool.sem_inc(lo_late, STAGES)
            pool.wait_ge(small_in, 80)
            pool.wait_ge(mv_done, NT)
            pool.tensor_scalar(rstd[:, 0, :], mv[:, :, 1], EPS, None, ALU.add).then_inc(pool_ve, 1)
            pool.wait_ge(pool_ve, 1)
            pool.tensor_tensor(rstd[:, 1, :], rstd[:, 0, :], k("minus_half"), ALU.pow).then_inc(rstd_done, 1)
            pool.memset(zpad[:], 0.0).then_inc(pad_done, 1)
            pool.wait_ge(pad_done, 1)
            pool.memset(zpad[:, C:C + 1], FAR).then_inc(pad_done, 1)
            with pool.Fori(0, LOOPED // STAGES) as g:
                for j in range(STAGES):
                    src, hi, lo = expert_chunk(g, j)
                    pool.wait_ge(hi_made, g * STAGES + (STAGES + j + 1))
                    pool.tensor_tensor(lo, staged(j, hi), hi.bitcast(F32), ALU.subtract).then_inc(lo_late, 1)
            pool.wait_ge(pad_done, 2)

            def send(n):
                if n < 2 * NT:
                    at, src, signal = where[:, n % 2, n // 2:n // 2 + 1], rows[:, n // 2, :], scattered
                else:
                    n -= 2 * NT
                    at, src, signal = where_pad[:, n:n + 1], zpad, y_out[n % 2] if n < 4 else scattered
                pool.indirect_dma_start(slots_dram, bass.IndirectOffsetOnAxis(ap=at, axis=0), src, None,
                                        bounds_check=SLOTS - 1, oob_is_err=False).then_inc(signal, 16)

            def batch(b, routed, sends):
                m0 = (b - BLIND) * TILES_B
                for kind, i in plan_of(b, routed):
                    if kind == "route":
                        pool.wait_ge(route_done, 1)
                        pool.wait_ge(rows_done, B)
                        places_known.append(True)
                    for n in itertools.islice(sends, SENDS.get(kind, 0) if places_known else 0):
                        send(n)
                    if kind == "turn":
                        pool.wait_ge(p_h, b * 2 + i + 1)
                        pool.tensor_tensor(phl[:, :, :, 1, :], prb[:], phl[:, :, :, 0, :].bitcast(F32),
                                           ALU.subtract).then_inc(p_l, 1)
                    if kind == "pv" and i % ND and routed:
                        h, d = i // ND, i % ND
                        n = h * (ND - 1) + d - 1
                        lo = DIST[d]
                        if d == 1:
                            drained(pool, None, b, "pv", i - 1)
                        pool.wait_ge(part_added, (b - h) * ADDS + n + 2)
                        drained(pool, None, b, "pv", i)
                        pool.tensor_tensor(acc[:, h, lo:T], acc[:, h, lo:T], part[:, n % 2, lo:T],
                                           ALU.add).then_inc(part_added, 1)
                    if kind == "down":
                        m = m0 + i
                        pool.wait_ge(home_done, m + 3)
                        pool.wait_ge(y_made, m + 2)
                        pool.sem_inc(pool_turn, 1)
                        pool.indirect_dma_start(
                            routed_dram, bass.IndirectOffsetOnAxis(ap=home[:, i % 4:i % 4 + 1], axis=0),
                            ys[:, i % 2, :], None, bounds_check=2 * NT * P - 1, oob_is_err=False)\
                            .then_inc(y_out[i % 2], 16)

            sends, places_known = iter(range(2 * NT + E + TAIL)), []
            for b in range(BLIND):
                batch(b, False, sends)
            for n in sends:
                send(n)
            with pool.Fori(BLIND, B) as b:
                batch(b, True, iter(()))
            batch(B, False, iter(()))
            with pool.Fori(0, B // SETS) as g:
                for n in range(SETS):
                    b = g * SETS + n
                    cx, cy, co = comb(n)
                    pool.wait_ge(silu_done, b + 1)
                    pool.tensor_tensor(co, co, xnt[:, bass.ds(b, 1), :].rearrange("p a (t c) -> p (a t) c", c=C),
                                       ALU.mult).then_inc(sg_done, 1)

        @block.scalar
        def _(act):
            def wait(s, v):
                hold(act, act_turn, s, v)

            act.sem_inc(xt_done, 2 * CH * 2)
            act.sem_inc(gelu_done, 1)
            act.sem_inc(y_made, 1)

            for j, (src, hi, lo) in enumerate(dense_chunks):
                act.wait_ge(raw_in[j], 16)
                act.activation(hi, staged(j, hi), ACT.Copy).then_inc(hi_made, 1)
            with act.Fori(0, B // 2) as g:
                for n in range(2):
                    b = g * 2 + n
                    wait(t_done, b * CH + 3 * CH)
                    wait(logit_done, b + 1)
                    for c in range(CH):
                        act.activation(xt_f[n][:, c, :], xt_bank[n][c][:], ACT.Copy).then_inc(xt_done, 1)
                    for c in range(CH):
                        act.activation(xnt[:, bass.ds(b, 1), c * T:(c + 1) * T].rearrange("p a n -> p (a n)"),
                                       xt_bank[n][c][:], ACT.Copy).then_inc(xt_done, 1)
                for j in range(STAGES):
                    src, hi, lo = expert_chunk(g, j)
                    wait(raw_in[j], g * 16 + 32)
                    act.activation(hi, staged(j, hi), ACT.Copy).then_inc(hi_made, 1)
            for j in range(2):
                hi = spread_chunk(j)[1]
                act.wait_ge(raw_in[j], 16 * (LOOPED // STAGES + 2))
                act.activation(hi, staged(j, hi), ACT.Copy).then_inc(hi_made, 1)
            def batch(b, routed):
                def full(kind, i, j=0):
                    k, n = bank_use(b, kind, i, j)
                    wait(d_full[k], n + 1)
                    return bank_d[k], d_free[k]

                m0 = (b - BLIND) * TILES_B
                for kind, i in plan_of(b, routed):
                    if kind == "route":
                        act.wait_ge(gap_done, 1)
                        act.activation(weight[:, 1, :], rk[7][:, 0:NT], ACT.Exp).then_inc(exp_done, 1)
                    if kind == "split":
                        act.activation(t_h[:].rearrange("p c n -> p (c n)"),
                                       xnt[:, bass.ds(b, 1), :].rearrange("p a n -> p (a n)"), ACT.Copy).then_inc(split_h, 1)
                    if kind == "qkv":
                        half, which = divmod(i, 3)
                        src, free = full(kind, i)
                        act.activation(qkv[:, 6 if i == 5 else i, :], src[:], ACT.Identity,
                                       bias=bqkv[:, which * CH + half:which * CH + half + 1]).then_inc(free, 1)
                    if kind == "v_move":
                        drained(act, act_turn, b, "qkv", 5)
                        if not (isinstance(b, int) and b == 0):
                            drained(act, act_turn, b, "pv", 2 * ND - 1)
                        act.activation(qkv[:, 5, :], qkv[:, 6, :], ACT.Copy).then_inc(v_moved, 1)
                    if kind == "shared_up":
                        src, free = full(kind, i)
                        act.activation(hs[:, i, :], src[:], ACT.Gelu, bias=bs1[:, i:i + 1]).then_inc(free, 1)
                    if kind == "hs_split":
                        for j in range(2):
                            drained(act, act_turn, b, "shared_up", j)
                        act.activation(t_h[:], hs, ACT.Copy).then_inc(hs_h, 1)
                    if kind == "shared_down":
                        src, free = full(kind, i)
                        if not routed and b:
                            wait(sh_stored[i], 16 * b)
                        dst = shared_at(b, 2 * i * C, 2 * C) if routed else sh_blind[i]
                        act.activation(dst, src[:], ACT.Copy).then_inc(free, 1)
                    if kind == "score_turn":
                        wait(prod_used, b * 2 * ND + (i + 1) * ND + RING)
                        act.activation(score_t[0:ND * HH, :], bank_s[0:ND * HH, :], ACT.Copy).then_inc(sums_out, 1)
                    if kind == "soft_norm":
                        wait(shifted, b * 2 + i + 1)
                        act.activation(prb[:], sco[:], ACT.Exp, scale=SCALE).then_inc(exped, 1)
                    if kind == "turn":
                        wait(normed, b * 2 + i + 1)
                        act.activation(phl[:, :, :, 0, :], prb[:], ACT.Copy).then_inc(p_h, 1)
                        for j in range(2):
                            src, free = full(kind, i, j)
                            act.activation(turned[:, i, j, :], src[:], ACT.Copy).then_inc(free, 1)
                    if kind == "mix_split":
                        wait(part_added, b * ADDS + 2)
                        act.activation(t_h[:], acc[:], ACT.Copy).then_inc(mix_h, 1)
                    if kind == "project":
                        src, free = full(kind, i)
                        act.activation(xnt[:, bass.ds(b - 1, 1), i * T:(i + 1) * T].rearrange("p a n -> p (a n)"),
                                       src[:], ACT.Copy).then_inc(free, 1)
                    m = m0 + i
                    if kind == "tx":
                        wait(tx_done, m + 3)
                        wait(up_done, m + 1)
                        act.activation(xs_h[:].rearrange("p c n -> p (c n)"), bank_tx[:, 0:C], ACT.Copy).then_inc(xs_hi, 1)
                        if i % 2 == 0:
                            wait(down_done, m + 2)
                            act.activation(pick[:, i % 4:i % 4 + 2, :],
                                           tile_row[:, bass.ds(m, 2)].rearrange("p (a n) -> p a n", n=1).to_broadcast([16, 2, P]),
                                           ACT.Copy).then_inc(pick_done, 1)
                    if kind == "up":
                        wait(up_done, m + 2)
                        wait(th_done, m + 1)
                        act.activation(hr, bank_up[:, 0:C], ACT.Gelu).then_inc(gelu_done, 1)
                    if kind == "th":
                        wait(th_done, m + 2)
                        wait(down_done, m + 4)
                        act.activation(hr_h[:].rearrange("p c n -> p (c n)"), bank_th[:, 0:C], ACT.Copy).then_inc(hr_hi, 1)
                    if kind == "down":
                        wait(down_done, m + 5)
                        wait(y_out[i % 2], 16 * ((b - BLIND) * (TILES_B // 2) + i // 2 + 2))
                        act.activation(ys[:, i % 2, :], bank_down[:, 0:C], ACT.Copy).then_inc(y_made, 1)

            for b in range(BLIND):
                batch(b, False)
            act.wait_ge(scattered, 16 * (2 * NT + E + TAIL - 4))
            for n in range(2):
                act.wait_ge(y_out[n], 32)
            for n in range(2):
                act.wait_ge(sh_stored[n], 16 * BLIND)
            with act.Fori(BLIND, B) as b:
                batch(b, True)
            batch(B, False)

            for n in range(SETS):
                act.sem_inc(c_out[n], 16)
            with act.Fori(0, B // SETS) as g:
                def store(n):
                    wait(o_made, g * SETS + n + 1)
                    act.dma_start(out_b[bass.ds(g * SETS + n, 1)].rearrange("a p t c -> p (a t) c"), comb(n)[2])\
                        .then_inc(c_out[n], 16)

                for n in range(SETS):
                    cx, cy, co = comb(n)
                    wait(g_parts, (g * SETS + n) * 8 + 8)
                    act.activation(co, co, ACT.Silu).then_inc(silu_done, 1)
                    if n:
                        store(n - 1)
                store(SETS - 1)

        @block.vector
        def _(dve):
            count = [0]

            def step(ins, base=None):
                count[0] += 1
                ins.then_inc(dve_done, 1)
                dve.wait_ge(dve_done, count[0] if base is None else base + count[0])

            dve.sem_inc(part_added, 2)
            dve.sem_inc(lg_done, 2)

            def mv_of(b, t, what):
                return mv[:, bass.ds(b * TT + t, 1), 0] if what == 0 else rstd[:, 1, bass.ds(b * TT + t, 1)]

            dve.wait_ge(small_in, 80)
            dve.wait_ge(brow_in, 32)
            for j, raw in enumerate((sco, prb)):
                r = raw[0:16].rearrange("p a b c -> p (a b c)")[:, 0:C]
                dst = brow[:, j * C:(j + 1) * C]
                tmp = part[0:16, 0, j * C:(j + 1) * C]
                step(dve.tensor_copy(dst, r))
                step(dve.tensor_tensor(tmp, r, dst.bitcast(F32), ALU.subtract))
                step(dve.tensor_scalar(tmp, tmp, k("row_lo")[0:16], None, ALU.mult))
                step(dve.scalar_tensor_tensor(dst, dst.bitcast(F32), k("row_hi")[0:16], tmp, ALU.mult, ALU.add))
            step(dve.tensor_scalar(part[0:16, 0, 0:P], k("ones")[0:16], k("row_expert")[0:16], None, ALU.mult))
            step(dve.tensor_scalar(dense_pick[:], part[0:16, 0, 0:P], -1.0, None, ALU.is_equal))
            before = count[0]

            for b in range(B):
                dve.wait_ge(x_in[b], 16)
                if b:
                    dve.wait_ge(mv_done, b * TT)
                for t in range(TT):
                    count[0] += 1
                    dve.bn_stats(stats[:, t, :], rows[:, b * TT + t, 0:C]).then_inc(dve_done, 1)
                dve.wait_ge(dve_done, count[0])
                for t in range(TT):
                    dve.bn_aggr(mv[:, b * TT + t, :], stats[:, t, :]).then_inc(mv_done, 1)
            for j, (src, hi, lo) in enumerate(dense_chunks):
                dve.wait_ge(hi_made, j + 1)
                dve.tensor_tensor(lo, staged(j, hi), hi.bitcast(F32), ALU.subtract).then_inc(lo_early, 1)
            dve.wait_ge(mv_done, NT)
            dve.wait_ge(rstd_done, 1)

            def logits(b, n):
                dve.wait_ge(logit_done, b + 3)
                dve.tensor_tensor(lg[:, bass.ds(b * TT, TT), :],
                                  logit_bank[n][:, 0:TT * 8].rearrange("p (t e) -> p t e", e=8)[:, :, 0:E],
                                  ebias[:].rearrange("p (a e) -> p a e", a=1).to_broadcast([P, TT, E]), ALU.add)\
                    .then_inc(lg_done, 1)

            def row_tile(b, t):
                return rows[:, bass.ds(b * TT + t, 1), 0:C].rearrange("p a n -> p (a n)")

            def normalise(g):
                for n in range(2):
                    b = g * 2 + n
                    dve.wait_ge(t_done, b * CH + CH)
                    for t in range(TT):
                        dve.tensor_scalar(xr[n][:, t, :], row_tile(b, t), mv_of(b, t, 0), mv_of(b, t, 1),
                                          ALU.subtract, ALU.mult).then_inc(xr_done, 1)

            def normalise_in_place(g):
                for n in range(2):
                    b = g * 2 + n
                    dve.wait_ge(xr_done, b * TT + TT)
                    for t in range(TT):
                        ins = dve.tensor_scalar(row_tile(b, t), row_tile(b, t), mv_of(b, t, 0), mv_of(b, t, 1),
                                                ALU.subtract, ALU.mult)
                    ins.then_inc(rows_done, 1)

            normalise(0)
            normalise_in_place(0)
            with dve.Fori(1, B // 2) as g:
                normalise(g)
                for n in range(2):
                    logits(g * 2 - 2 + n, n)
                normalise_in_place(g)
            for n in range(2):
                logits(B - 2 + n, n)

            base_n = count[0]

            routed_steps = [0]

            def route_step(ins):
                routed_steps[0] += 1
                ins.then_inc(route_steps, 1)
                dve.wait_ge(route_steps, routed_steps[0])

            def route():
                dve.wait_ge(lg_done, B + 2)
                dve.wait_ge(rows_done, B)
                dve.wait_ge(lo_late, LOWS)
                dve.wait_ge(hi_made, LOWS + 2)

                def te(a):
                    return a[:, 0:NT * E].rearrange("p (t e) -> p t e", e=E)

                def row_e(a):
                    return a.rearrange("p (a e) -> p a e", a=1).to_broadcast([P, NT, E])

                rank, win, sel1, sel2, slot, tmp, total = map(te, rk[0:7])
                small = rk[7]
                route_step(dve.tensor_copy(rank, row_e(k("rank0"))))
                for s in range(1, E):
                    route_step(dve.tensor_tensor(win[:, :, 0:E - s], lg[:, :, 0:E - s], lg[:, :, s:E], ALU.is_ge))
                    route_step(dve.tensor_tensor(rank[:, :, s:E], rank[:, :, s:E], win[:, :, 0:E - s], ALU.add))
                    route_step(dve.tensor_tensor(rank[:, :, 0:E - s], rank[:, :, 0:E - s], win[:, :, 0:E - s], ALU.subtract))
                route_step(dve.tensor_scalar(sel1, rank, 0.0, None, ALU.is_equal))
                route_step(dve.tensor_scalar(sel2, rank, 1.0, None, ALU.is_equal))
                dve.tensor_tensor(win, sel1, sel2, ALU.add).then_inc(rank_done, 1)
                dve.wait_ge(rank_done, 1)
                route_step(dve.tensor_tensor(tmp, sel2, lg, ALU.mult))
                route_step(dve.tensor_reduce(weight[:, 1, :], tmp, AX.X, ALU.add))
                route_step(dve.tensor_reduce(weight[:, 0, :], lg, AX.X, ALU.max))
                dve.tensor_tensor(small[:, 0:NT], weight[:, 1, :], weight[:, 0, :], ALU.subtract).then_inc(gap_done, 1)
                route_step(dve.tensor_tensor(tmp, sel1, row_e(k("expert")), ALU.mult))
                route_step(dve.tensor_reduce(rows[:, :, C + 1:C + 2].rearrange("p t a -> p (t a)"), tmp, AX.X, ALU.add))
                route_step(dve.tensor_copy(rows[:, :, C:C + 1].rearrange("p t a -> p (t a)"), k("token2")))
                dve.wait_ge(count_done, 2)
                route_step(dve.tensor_copy(total, te(bank_tx)))
                for e in range(E):
                    route_step(dve.tensor_tensor_scan(tmp[:, :, e], k("ones")[:, 0:NT], total[:, :, e], 0.0, ALU.mult, ALU.add))
                cnt = small[:, 32:32 + E]
                tiles = small[:, 40:40 + E]
                end = small[:, 48:48 + E]
                base = small[:, 56:56 + E]
                over = small[:, 64:64 + E]
                pad = small[:, 80:80 + E + TAIL]
                route_step(dve.tensor_copy(cnt, tmp[:, NT - 1, :]))
                route_step(dve.tensor_tensor(slot, tmp, total, ALU.subtract))
                route_step(dve.tensor_tensor(slot, slot, te(bank_s), ALU.add))
                et = rk[1][:, 0:E * NT].rearrange("p (e t) -> p e t", t=NT)
                route_step(dve.tensor_tensor(et, cnt.rearrange("p (e a) -> p e a", a=1).to_broadcast([P, E, NT]),
                                       k("edges").rearrange("p (a t) -> p a t", a=1).to_broadcast([P, E, NT]), ALU.is_gt))
                route_step(dve.tensor_reduce(tiles, et, AX.X, ALU.add))
                route_step(dve.tensor_tensor_scan(end, k("ones")[:, 0:E], tiles, 0.0, ALU.mult, ALU.add))
                route_step(dve.tensor_tensor(base, end, tiles, ALU.subtract))
                route_step(dve.tensor_scalar(base, base, float(P), None, ALU.mult))
                route_step(dve.tensor_tensor(slot, slot, row_e(base), ALU.add))
                for j, sel in enumerate((sel1, sel2)):
                    route_step(dve.tensor_tensor(tmp, sel, slot, ALU.mult))
                    route_step(dve.tensor_reduce(rk[1][:, j * NT:(j + 1) * NT], tmp, AX.X, ALU.add))
                    route_step(dve.tensor_copy(where[:, j, :], rk[1][:, j * NT:(j + 1) * NT]))
                je = prod[:, 2, 0:RT * E].rearrange("p (j e) -> p j e", e=E)
                route_step(dve.tensor_tensor(je, k("tile_no").rearrange("p (j a) -> p j a", a=1).to_broadcast([P, RT, E]),
                                       end.rearrange("p (a e) -> p a e", a=1).to_broadcast([P, RT, E]), ALU.is_ge))
                route_step(dve.tensor_reduce(tile_ef[:], je, AX.X, ALU.add))
                route_step(dve.tensor_scalar(tile_ef[:], tile_ef[:], float(E - 1), None, ALU.min))
                packed = rk[0][0:1, 0:RT].rearrange("p (a n) -> p a n", n=PACK)
                route_step(dve.tensor_tensor(packed, tile_ef[0:1, :].rearrange("p (a n) -> p a n", n=PACK),
                                       k("octal")[0:1].rearrange("p (a n) -> p a n", a=1).to_broadcast([1, RT // PACK, PACK]),
                                       ALU.mult))
                route_step(dve.tensor_reduce(rk[0][0:1, 128:128 + RT // PACK], packed, AX.X, ALU.add))
                route_step(dve.tensor_copy(tile_ei[:], rk[0][0:1, 128:128 + RT // PACK]))
                route_step(dve.tensor_scalar(tile_row[:], tile_ef[0:16, :], k("row_expert")[0:16], None, ALU.is_equal))
                route_step(dve.tensor_scalar(end, end, float(P), None, ALU.mult))
                route_step(dve.tensor_tensor(pad[:, 0:E], base, cnt, ALU.add))
                route_step(dve.tensor_scalar(pad[:, 0:E], pad[:, 0:E], k("lane"), None, ALU.add))
                route_step(dve.tensor_tensor(over, pad[:, 0:E], end, ALU.is_ge))
                route_step(dve.scalar_tensor_tensor(pad[:, 0:E], over, FAR, pad[:, 0:E], ALU.mult, ALU.add))
                route_step(dve.tensor_scalar(pad[:, E:], k("tail"), end[:, E - 1:E], None, ALU.add))
                route_step(dve.tensor_copy(where_pad[:], pad))
                dve.wait_ge(exp_done, 1)
                route_step(dve.tensor_scalar(small[:, 0:NT], weight[:, 1, :], 1.0, None, ALU.add))
                route_step(dve.reciprocal(weight[:, 0, :], small[:, 0:NT]))
                dve.tensor_tensor(weight[:, 1, :], weight[:, 1, :], weight[:, 0, :], ALU.mult).then_inc(route_done, 1)
                dve.wait_ge(route_done, 1)
                dve.sem_inc(s_free, 1)
            def batch(b, routed, per, start):
                count[0] = 0
                origin = b * per + start

                def mark(ins):
                    step(ins, origin)

                def full(kind, i):
                    k, n = bank_use(b, kind, i)
                    dve.wait_ge(d_full[k], n + 1)
                    return bank_d[k], d_free[k]

                m0 = (b - BLIND) * TILES_B
                for kind, i in plan_of(b, routed):
                    m = m0 + i
                    if kind == "route":
                        route()
                    if kind == "split":
                        dve.wait_ge(split_h, b + 1)
                        dve.tensor_tensor(t_l[:].rearrange("p c n -> p (c n)"),
                                          xnt[:, bass.ds(b, 1), :].rearrange("p a n -> p (a n)"),
                                          t_h[:].rearrange("p c n -> p (c n)").bitcast(F32), ALU.subtract)\
                            .then_inc(split_l, 1)
                    if kind == "product":
                        h, d = divmod(i, ND)
                        if i == 1:
                            dve.wait_ge(hs_l, b + 1)
                        if d == 0:
                            for j in range(2):
                                drained(dve, None, b, "qkv", 3 * h + j)
                        lo = DIST[d]
                        dve.wait_ge(prod_used, b * 2 * ND + max(i + 1, RING))
                        dve.tensor_tensor(product_at(i)[:, lo:T], qkv[:, 3 * h, lo:T], qkv[:, 3 * h + 1, 0:T - lo],
                                          ALU.mult).then_inc(prod_ready, 1)
                    if kind == "soft_max":
                        dve.wait_ge(s_full, b * 2 + i + 1)
                        s4 = bank_s[:, 0:TT * ND * HH].rearrange("p (t d h) -> p t d h", d=ND, h=HH)
                        msk = k("mask").rearrange("p (t d a) -> p t d a", d=ND, a=1).to_broadcast([P, TT, ND, HH])
                        dve.tensor_tensor(sco[:], s4, msk, ALU.add).then_inc(s_free, 1)
                        dve.wait_ge(s_free, b * 2 + i + 2)
                        mark(dve.tensor_reduce(red[:, 0], sco[:].rearrange("p t d h -> p t h d"), AX.X, ALU.max))
                        dve.tensor_tensor(sco[:], sco[:],
                                          red[:, 0:1].rearrange("p a t h -> p t a h").to_broadcast([P, TT, ND, HH]),
                                          ALU.subtract).then_inc(shifted, 1)
                    if kind == "soft_norm":
                        dve.wait_ge(exped, b * 2 + i + 1)
                        mark(dve.tensor_reduce(red[:, 1], prb[:].rearrange("p t d h -> p t h d"), AX.X, ALU.add))
                        mark(dve.reciprocal(red[:, 2], red[:, 1]))
                        dve.tensor_tensor(prb[:], prb[:],
                                          red[:, 2:3].rearrange("p a t h -> p t a h").to_broadcast([P, TT, ND, HH]),
                                          ALU.mult).then_inc(normed, 1)
                    if kind == "hs_split":
                        dve.wait_ge(hs_h, b + 1)
                        dve.tensor_tensor(t_l[:], hs, t_h[:].bitcast(F32), ALU.subtract).then_inc(hs_l, 1)
                    if kind == "pv":
                        h, d = i // ND, i % ND
                        lo = DIST[d]
                        src, free = full(kind, i)
                        if d == 0:
                            if h == 0:
                                dve.wait_ge(mix_l, b + 1)
                                drained(dve, None, b, "qkv", 2)
                            else:
                                dve.wait_ge(v_moved, b)
                            dve.tensor_tensor(acc[:, h, :], src[:], qkv[:, 3 * h + 2, :], ALU.mult).then_inc(free, 1)
                        else:
                            n = h * (ND - 1) + d - 1
                            dve.wait_ge(part_added, (b - h) * ADDS + n + 1)
                            at = lo % 2
                            dve.tensor_tensor(part[:, n % 2, lo:T], src[:, at:at + T - lo], qkv[:, 3 * h + 2, 0:T - lo],
                                              ALU.mult).then_inc(free, 1)
                        for j in range(max(i - 1, ND * h + 1), i if d < ND - 1 else i + 1) if not routed else ():
                            n, lo = h * (ND - 1) + j % ND - 1, DIST[j % ND]
                            if j % ND == 1:
                                drained(dve, None, b, "pv", j - 1)
                            dve.wait_ge(part_added, (b - h) * ADDS + n + 2)
                            drained(dve, None, b, "pv", j)
                            dve.tensor_tensor(acc[:, h, lo:T], acc[:, h, lo:T], part[:, n % 2, lo:T],
                                              ALU.add).then_inc(part_added, 1)
                    if kind == "mix_split":
                        dve.wait_ge(mix_h, b)
                        dve.tensor_tensor(t_l[:], acc[:], t_h[:].bitcast(F32), ALU.subtract).then_inc(mix_l, 1)
                    if kind == "tx":
                        dve.wait_ge(xs_in[i % 2], 16 * ((b - BLIND) * (TILES_B // 2) + i // 2 + 1))
                        dve.wait_ge(home_done, m + 2)
                        dve.tensor_tensor(homef[:, 0:1], xs[:, i % 2, C + 1:C + 2], tile_ef[:, bass.ds(m, 1)],
                                          ALU.not_equal).then_inc(home_f, 1)
                        dve.wait_ge(home_f, m + 1)
                        dve.wait_ge(y_out[i % 2], 16 * ((b - BLIND) * (TILES_B // 2) + i // 2 + 1))
                        dve.tensor_tensor(home[:, i % 4:i % 4 + 1], homef[:, 0:1], xs[:, i % 2, C:C + 1],
                                          ALU.add).then_inc(home_done, 1)
                        dve.wait_ge(xs_hi, m + 1)
                        dve.tensor_tensor(xs_l[:].rearrange("p c n -> p (c n)"), bank_tx[:, 0:C],
                                          xs_h[:].rearrange("p c n -> p (c n)").bitcast(F32), ALU.subtract)\
                            .then_inc(xs_lo, 1)
                    if kind == "th":
                        dve.wait_ge(hr_hi, m + 1)
                        dve.tensor_tensor(hr_l[:].rearrange("p c n -> p (c n)"), bank_th[:, 0:C],
                                          hr_h[:].rearrange("p c n -> p (c n)").bitcast(F32), ALU.subtract)\
                            .then_inc(hr_lo, 1)
                return count[0]

            dve.sem_inc(home_done, 2)
            dve.sem_inc(xs_lo, 1)
            dve.sem_inc(hr_lo, 1)
            dve.sem_inc(mix_l, 1)
            per = 2 * 3
            for b in range(BLIND):
                assert batch(b, False, per, base_n) == per
            with dve.Fori(BLIND, B) as b:
                assert batch(b, True, per, base_n) == per
            batch(B, False, per, base_n)

            dve.wait_ge(sh_back, 16 * BLIND)
            with dve.Fori(0, B // SETS) as g:
                def add(n):
                    cx, cy, co = comb(n)
                    dve.wait_ge(sg_done, g * SETS + n + 1)
                    dve.tensor_tensor(co, co, cx, ALU.add).then_inc(o_made, 1)

                for n in range(SETS):
                    b = g * SETS + n
                    cx, cy, co = comb(n)
                    dve.wait_ge(c_in[n], g * 32 + 32)
                    for j in range(2):
                        for t in range(TT):
                            w = weight[:, j, bass.ds(b * TT + t, 1)]
                            y = cy[:, t, j * C:(j + 1) * C]
                            other = shared_at(b, t * C, C) if j == 0 else co[:, t, :]
                            dve.scalar_tensor_tensor(co[:, t, :], y, w, other, ALU.mult, ALU.add).then_inc(g_parts, 1)
                        dve.wait_ge(g_parts, b * 8 + j * 4 + 4)
                    if n:
                        add(n - 1)
                add(SETS - 1)

        @block.tensor
        def _(pe):
            for i in range(BANKS):
                pe.sem_inc(d_free[i], 1)
            pe.sem_inc(logit_done, 2)
            pe.sem_inc(t_done, 2 * CH)
            pe.sem_inc(prod_used, RING)
            pe.sem_inc(tx_done, 2)
            pe.sem_inc(up_done, 1)
            pe.sem_inc(th_done, 1)
            pe.sem_inc(down_done, 4)
            pe.wait_ge(small_in, 80)
            with pe.Fori(0, B // 2) as g:
                for n in range(2):
                    b = g * 2 + n
                    pe.wait_ge(xr_done, b * TT + TT)
                    pe.wait_ge(xt_done, b * 2 * CH + 2 * CH)
                    for c in range(CH):
                        for t in range(TT):
                            last = pe.transpose(xt_bank[n][c][:, t * P:(t + 1) * P], xr[n][:, t, c * P:(c + 1) * P],
                                                ident)
                        last.then_inc(t_done, 1)
                for n in range(2):
                    b = g * 2 + n
                    pe.wait_ge(xt_done, b * 2 * CH + 4 * CH + CH)
                    pe.wait_ge(lg_done, b + 1)
                    for t in range(TT):
                        for c in range(CH):
                            last = pe.matmul(logit_bank[n][:, t * 8:t * 8 + E], xt_f[n][:, c, t * P:(t + 1) * P],
                                             gate[:, c, :], start=c == 0, stop=c == CH - 1)
                    last.then_inc(logit_done, 1)
            pe.wait_ge(xt_done, B * 2 * CH + 4 * CH)
            pe.wait_ge(lo_early, STAGES)
            pe.wait_ge(lo_late, LOWS)
            pe.wait_ge(hi_made, LOWS + 2)

            def three(dst, left, right, first=True, last=True):
                n = 0
                for c in range(CH):
                    for a, w in ((0, 0), (0, 1), (1, 0)):
                        mm = pe.matmul(dst, left[a](c), right[w](c), start=first and n == 0,
                                       stop=last and n == 3 * CH - 1)
                        n += 1
                return mm

            def batch(b, routed):
                def take(kind, i, j=0):
                    k, n = bank_use(b, kind, i, j)
                    pe.wait_ge(d_free[k], n + 1)
                    return bank_d[k], d_full[k]

                m0 = (b - BLIND) * TILES_B
                experts = []
                for a in range(TILES_B // PACK if routed else 0):
                    packed = pe.value_load(tile_ei[0:1, bass.ds((b - BLIND) * (TILES_B // PACK) + a, 1)],
                                           min_val=0, max_val=8 ** PACK - 1)
                    experts += [pe.snap((packed >> (3 * i)) & 7) for i in range(PACK)]
                for kind, i in plan_of(b, routed):
                    m = m0 + i
                    if kind == "route":
                        pe.wait_ge(rank_done, 1)
                        win = rk[1][:, 0:NT * E]
                        pe.matmul(bank_s[:, 0:NT * E], k("before"), win, start=True, stop=True).then_inc(count_done, 1)
                        pe.matmul(bank_tx[:, 0:NT * E], k("ones"), win, start=True, stop=True).then_inc(count_done, 1)
                    if kind == "qkv":
                        half, which = divmod(i, 3)
                        col = which * C + half * P
                        dst, fullsem = take(kind, i)
                        three(dst[:], [lambda c: wqkv_h[:, c, col:col + P], lambda c: wqkv_l[:, c, col:col + P]],
                              [lambda c: t_h[:, c, :], lambda c: t_l[:, c, :]]).then_inc(fullsem, 1)
                    if kind == "shared_up":
                        if i == 0:
                            pe.wait_ge(split_l, b + 1)
                        dst, fullsem = take(kind, i)
                        s = slice(i * P, (i + 1) * P)
                        three(dst[:], [lambda c: w1_h[:, SHARED, c, s], lambda c: w1_l[:, SHARED, c, s]],
                              [lambda c: t_h[:, c, :], lambda c: t_l[:, c, :]]).then_inc(fullsem, 1)
                    if kind in ("shared_down", "project"):
                        dst, fullsem = take(kind, i)
                        if kind == "project":
                            pe.wait_ge(mix_l, b + 1)
                            wh, wl = (lambda c: wp_h[:, c, :]), (lambda c: wp_l[:, c, :])
                        else:
                            pe.wait_ge(hs_l, b + 1)
                            wh, wl = (lambda c: w2_h[:, SHARED, c, :]), (lambda c: w2_l[:, SHARED, c, :])
                        bias = brow[:, 0:C] if kind == "project" else brow[:, C:2 * C]
                        for j in range(2):
                            s = slice((2 * i + j) * P, (2 * i + j + 1) * P)
                            o = dst[:, j * C:(j + 1) * C]
                            three(o, [lambda c: t_h[:, c, s], lambda c: t_l[:, c, s]], [wh, wl], last=False)
                            mm = pe.matmul(o, dense_pick[:], bias, start=False, stop=True)
                        mm.then_inc(fullsem, 1)
                    if kind == "score":
                        h, d = divmod(i, ND)
                        if d == 0:
                            pe.wait_ge(s_free, b * 2 + h + 1)
                        pe.wait_ge(prod_ready, b * 2 * ND + i + 1)
                        lo = DIST[d]
                        at = (ND - 1 - d) * HH
                        pe.matmul(bank_s[0:ND * HH, lo:T], k("head_sum")[:, at:at + ND * HH],
                                  product_at(i)[:, lo:T], start=d == 0, stop=d == ND - 1).then_inc(prod_used, 1)
                    if kind == "score_turn":
                        pe.wait_ge(sums_out, b * 2 + i + 1)
                        for t in range(TT):
                            at = t * ND * HH
                            mm = pe.transpose(bank_s[:, at:at + ND * HH], score_t[0:ND * HH, t * P:(t + 1) * P],
                                              ident[0:ND * HH, 0:ND * HH])
                        mm.then_inc(s_full, 1)
                    if kind == "turn":
                        pe.wait_ge(p_l, b * 2 + i + 1)
                        flat = phl[:].rearrange("p t d a h -> p t (d a h)").bitcast(F32)
                        for j in range(2):
                            dst, fullsem = take(kind, i, j)
                            n0 = (0, SECOND * 2 * HH)[j]
                            for t in range(TT):
                                mm = pe.transpose(dst[:, t * P:(t + 1) * P], flat[:, t, n0:n0 + P], ident)
                            mm.then_inc(fullsem, 1)
                    if kind == "pv":
                        h, d = i // ND, i % ND
                        if d == 0:
                            for j in range(2):
                                drained(pe, None, b - h, "turn", h, j)
                        dst, fullsem = take(kind, i)
                        lo = DIST[d] // 2 * 2
                        j, pick_d = (0, d) if d < 8 else (1, d - SECOND)
                        pe.matmul(dst[:, 0:T - lo], sp_r[:, pick_d, :], turned[:, h, j, lo:T], start=True, stop=True)\
                            .then_inc(fullsem, 1)
                    if kind == "tx":
                        pe.wait_ge(xs_in[i % 2], 16 * ((b - BLIND) * (TILES_B // 2) + i // 2 + 1))
                        pe.wait_ge(xs_lo, m + 1)
                        for c in range(CH):
                            mm = pe.transpose(bank_tx[:, c * P:(c + 1) * P], xs[:, i % 2, c * P:(c + 1) * P], ident)
                        mm.then_inc(tx_done, 1)
                    if kind == "th":
                        pe.wait_ge(gelu_done, m + 2)
                        pe.wait_ge(hr_lo, m + 1)
                        for c in range(CH):
                            mm = pe.transpose(bank_th[:, c * P:(c + 1) * P], hr[:, c * P:(c + 1) * P], ident)
                        mm.then_inc(th_done, 1)
                    if kind in ("up", "down"):
                        up = kind == "up"
                        e = experts[i]
                        l_h, l_l = (xs_h, xs_l) if up else (hr_h, hr_l)
                        r_h, r_l = (w1_h, w1_l) if up else (w2_h, w2_l)
                        o = (bank_up if up else bank_down)[:, 0:C]
                        if up:
                            pe.wait_ge(pick_done, (b - BLIND) * (TILES_B // 2) + i // 2 + 1)
                            pe.wait_ge(xs_lo, m + 2)
                            pe.wait_ge(gelu_done, m + 1)
                        else:
                            pe.wait_ge(hr_lo, m + 2)
                            pe.wait_ge(y_made, m + 1)
                        pe.matmul(o, pick[:, i % 4, :], brow[:, 0:C] if up else brow[:, C:2 * C], start=True, stop=False)

                        def moving(r):
                            return lambda c: r[:, bass.ds(e, 1), c, :].rearrange("p a n -> p (a n)")
                        three(o, [lambda c: l_h[:, c, :], lambda c: l_l[:, c, :]], [moving(r_h), moving(r_l)],
                              first=False).then_inc(up_done if up else down_done, 1)

            for b in range(BLIND):
                batch(b, False)
            pe.wait_ge(route_done, 1)
            with pe.Fori(BLIND, B) as b:
                batch(b, True)
            batch(B, False)


def kernel(L0_attn_x, L0_attn_W_qkv, L0_attn_b_qkv, L0_attn_W_proj, L0_attn_b_proj, L0_ffn_gate_w,
           L0_ffn_expert_bias, L0_ffn_sw1, L0_ffn_sb1, L0_ffn_sw2, L0_ffn_sb2, L0_ffn_rw1, L0_ffn_rb1,
           L0_ffn_rw2, L0_ffn_rb2):
    import concourse.bacc as bacc
    from concourse.bass_utils import run_bass_kernel_spmd

    a = {k: np.asarray(v) for k, v in dict(
        x=L0_attn_x, w_qkv=L0_attn_W_qkv, w_proj=L0_attn_W_proj, expert_bias=L0_ffn_expert_bias).items()}
    a["b_qkv"] = np.asarray(L0_attn_b_qkv).reshape(-1, P).T
    a["sb1"] = np.asarray(L0_ffn_sb1).reshape(-1, P).T
    a["gate_t"] = np.asarray(L0_ffn_gate_w).T
    a["w1"] = np.concatenate([np.asarray(L0_ffn_rw1), np.asarray(L0_ffn_sw1)[None]])
    a["w2"] = np.concatenate([np.asarray(L0_ffn_rw2), np.asarray(L0_ffn_sw2)[None]])
    routed = np.concatenate([np.asarray(L0_ffn_rb1), np.asarray(L0_ffn_rb2)], axis=1)
    dense = np.concatenate([np.asarray(L0_attn_b_proj), np.asarray(L0_ffn_sb2)])[None]
    a["bias_rows"] = np.concatenate([routed, routed, dense, dense])
    a["consts"], a["spread"] = constants()

    nc = bacc.Bacc("TRN2", target_bir_lowering=False, num_devices=1, dynamic_dma_scratch_size=7168)
    arrays, args = {}, {}
    for name, v in a.items():
        arrays[f"in_{name}"] = np.ascontiguousarray(v)
        args[name] = nc.dram_tensor(f"in_{name}", v.shape, F32, kind="ExternalInput").ap()
    args["out"] = nc.dram_tensor("out_x", (B, T, C), F32, kind="ExternalOutput").ap()
    args["slots_dram"] = nc.dram_tensor("slots", (SLOTS, ROW), F32, kind="Internal").ap()
    args["routed_dram"] = nc.dram_tensor("routed", (2 * B * T, C), F32, kind="Internal").ap()
    args["shared_dram"] = nc.dram_tensor("shared", (B * T, C), F32, kind="Internal").ap()
    build(nc, **args)
    r = run_bass_kernel_spmd(nc, [arrays], core_ids=[0])
    return r.results[0]["out_x"]
```

```python
from contextlib import ExitStack

import numpy as np

import concourse.bass as bass
from concourse import mybir

F32 = mybir.dt.float32
F32R = mybir.dt.float32r
U32 = mybir.dt.uint32
I32 = mybir.dt.int32
ALU = mybir.AluOpType
ACT = mybir.ActivationFunctionType
AX = mybir.AxisListType

P = 128
B, T, C = 8, 512, 256
HEADS = 16
DH = C // HEADS
TT = T // P
NT = B * TT
CH = C // P
HH = HEADS // CH
DIST = [0] + [1 << k for k in range(T.bit_length() - 1)]
ND = len(DIST)
ADDS = CH * (ND - 1)
E = 7
SHARED = E
EPS = 1e-5
SCALE = DH ** -0.5
ROW = C + 2
BLIND = 2
TILES_B = 12
RT = (B - BLIND) * TILES_B
SLOTS = RT * P
TAIL = SLOTS // P - 2 * NT
FAR = 1.0e6
SECOND = ND - 8
BANKS = 3
RING = 3
PACK = 6
STAGES = 4
AHEAD = 6
SETS = 4
assert RT >= 2 * NT + E - 1 and B & (B - 1) == 0

CONST = {}
_at = 0
for _name, _n in (("ident", P), ("head_sum", 2 * (ND - 1) * HH + HH), ("mask", TT * ND), ("before", P), ("ones", P),
                  ("edges", NT), ("tile_no", RT), ("lane", 1), ("rank0", E), ("expert", E),
                  ("token2", NT), ("row_expert", 1), ("row_hi", 1), ("row_lo", 1), ("octal", PACK),
                  ("minus_half", NT)):
    CONST[_name] = (_at, _n)
    _at += _n
NCONST = _at


def constants():
    c = np.zeros((P, NCONST), np.float32)
    p = np.arange(P)

    def put(name, v):
        at, n = CONST[name]
        c[:, at:at + n] = np.broadcast_to(np.asarray(v, np.float32), (P, n))

    put("ident", np.eye(P))
    put("head_sum", (p[:, None] // DH == np.arange(2 * (ND - 1) * HH + HH)[None, :] - (ND - 1) * HH))
    tok = np.arange(TT)[None, :, None] * P + p[:, None, None]
    put("mask", np.where(tok >= np.array(DIST)[None, None, :], 0.0, -1e30).reshape(P, -1))
    put("before", p[:, None] < p[None, :])
    put("ones", np.ones((1, P)))
    put("edges", np.arange(NT)[None] * P)
    put("tile_no", np.arange(RT)[None])
    put("lane", p[:, None])
    put("rank0", (E - 1 - np.arange(E))[None])
    put("expert", np.arange(E)[None])
    put("token2", 2 * (np.arange(NT)[None] * P + p[:, None]))
    put("row_expert", np.where(p < 2 * E, p % E, -1)[:, None])
    put("row_hi", ((p < E) | (p == 2 * E))[:, None])
    put("row_lo", (((p >= E) & (p < 2 * E)) | (p == 2 * E + 1))[:, None])
    put("octal", 8.0 ** np.arange(PACK)[None])
    put("minus_half", np.full((1, NT), -0.5))
    s = np.zeros((8, 2, HH, 8, P), np.float32)
    for d in range(8):
        for ch in range(P):
            s[d, :, ch // DH, d, ch] = 1.0
    return c, s.reshape(P, 8 * P)


ORDER = """
+ 1, -soft_norm 1, shared_up 0, shared_up 1, + 2, qkv 0, qkv 1, + 1, -turn 1, -pv 10, -pv 11, route 0
-pv 12, + 1, qkv 2, + 1, -pv 13, -pv 14, qkv 3, + 2, qkv 4, qkv 5, + 2, product 0, -pv 15, -pv 16, + 1
hs_split 0, score 0, product 1, + 1, product 2, + 2, -pv 17, score 1, product 3, + 1, -pv 18, product 4
score 2, score 3, -pv 19, product 5, + 1, score 4, product 6, shared_down 0, v_move 0, score 5, product 7
score 6, product 8, shared_down 1, product 9, + 1, score 7, score 8, -mix_split 0, score 9, + 1
product 10, score_turn 0, + 1, -project 0, -project 1, soft_max 0, product 11, score 10, product 12, + 2
product 13, soft_norm 0, score 11, score 12, product 14, + 3, score 13, turn 0, product 15, + 1, pv 0
+ 1, pv 1, + 1, score 14, product 16, + 1, pv 2, score 15, product 17, + 2, pv 3, score 16, next_split 0
+ 2, product 18, + 3, pv 4, score 17, product 19, + 3, pv 5, + 1, pv 6, score 18, + 5, score 19, + 3
pv 7, score_turn 1, pv 8, + 1, pv 9, soft_max 1
"""


def body_plan(own=True, before=True, routed=True):
    plan, tiles = [], []
    for i in range(TILES_B + 3 if routed else 0):
        tiles += [("down", i - 3)] if 0 <= i - 3 < TILES_B else []
        tiles += [("th", i - 2)] if 0 <= i - 2 < TILES_B else []
        tiles += [("up", i - 1)] if 0 <= i - 1 < TILES_B else []
        tiles += [("tx", i)] if i < TILES_B else []
    for stage in ORDER.strip().replace("\n", ",").split(","):
        kind, number = stage.split()
        if kind == "+":
            plan += tiles[:int(number)]
            del tiles[:int(number)]
        elif before if kind[0] == "-" else own and (kind != "route" or not before):
            plan.append((kind.lstrip("-"), int(number)))
    return plan


def bank_uses(plan):
    takes = dict(turn=2, qkv=1, shared_up=1, shared_down=1, pv=1, project=1)
    use, n = {}, 0
    for stage in plan:
        use[stage] = [n + j for j in range(takes.get(stage[0], 0))]
        n += len(use[stage])
    return use, n


PLAN_FIRST = body_plan(before=False, routed=False)
PLAN_BLIND = body_plan(routed=False)
PLAN_ROUTED = body_plan()
PLAN_LAST = body_plan(own=False, routed=False)
USE_FIRST, TAKEN_FIRST = bank_uses(PLAN_FIRST)
USE_MIDDLE, TAKEN = bank_uses(PLAN_ROUTED)
USE_LAST, _ = bank_uses(PLAN_LAST)
assert TAKEN % BANKS == 0


def plan_of(b, routed):
    return PLAN_ROUTED if routed else (PLAN_FIRST if b == 0 else PLAN_LAST if b == B else PLAN_BLIND)


def bank_use(b, kind, i, j=0):
    if isinstance(b, int) and b == 0:
        n = USE_FIRST[kind, i][j]
        return n % BANKS, n // BANKS
    n = TAKEN_FIRST + (USE_LAST if isinstance(b, int) and b == B else USE_MIDDLE)[kind, i][j]
    return n % BANKS, b * (TAKEN // BANKS) + (n - TAKEN) // BANKS


def build(nc, x, w_qkv, b_qkv, w_proj, bias_rows, gate_t, expert_bias, w1, w2, sb1, consts, spread,
          out, slots_dram, routed_dram, shared_dram):
    x_b = x.rearrange("b (t p) c -> b p t c", p=P)
    out_b = out.rearrange("b (t p) c -> b p t c", p=P)
    shared_b = shared_dram.rearrange("(b t p) c -> b p t c", p=P, t=TT)
    routed_b = routed_dram.rearrange("(b t p k) c -> b p t (k c)", p=P, t=TT, k=2)
    slots_t = slots_dram.rearrange("(j p) c -> j p c", p=P)

    with ExitStack() as ctx:
        def sb(name, shape, dt=F32):
            return ctx.enter_context(nc.sbuf_tensor(name, shape, dt))

        def bank(name):
            return ctx.enter_context(nc.psum_tensor(name, [P, 512], F32))

        def sem(name):
            return ctx.enter_context(nc.semaphore(name))

        rows = sb("rows", [P, NT, ROW])
        xnt = sb("xnt", [P, B, CH * T])
        wp_h, wp_l = sb("wp_h", [P, CH, C], F32R), sb("wp_l", [P, CH, C], F32R)
        sp_r = sb("sp_r", [P, 8, P], F32R)
        cst = sb("cst", [P, NCONST])
        bqkv = sb("bqkv", [P, 6])
        bs1 = sb("bs1", [P, CH])
        gate = sb("gate", [P, CH, E])
        ebias = sb("ebias", [P, E])
        brow = sb("brow", [16, 2 * C], F32R)
        dense_pick = sb("dense_pick", [16, P], F32R)
        t_h, t_l = sb("t_h", [P, CH, T], F32R), sb("t_l", [P, CH, T], F32R)
        qkv = sb("qkv", [P, 7, T])
        prod = sb("prod", [P, RING, T])
        part = sb("part", [P, 2, T])
        acc = sb("acc", [P, CH, T])
        sco = sb("sco", [P, TT, ND, HH])
        prb = sb("prb", [P, TT, ND, HH])
        phl = sb("phl", [P, TT, ND, 2, HH], F32R)
        hs = prod[:, 0:CH, :]
        score_t = prod[:, 2, :]
        red = sb("red", [P, 3, TT, HH])
        turned = sb("turned", [P, CH, 2, T], F32R)
        tile_in = sb("tile_in", [P, 2 * ROW + C])
        xs = tile_in[:, 0:2 * ROW].rearrange("p (a n) -> p a n", a=2)
        hr = tile_in[:, 2 * ROW:2 * ROW + C]
        xs_h, xs_l = sb("xs_h", [P, CH, P], F32R), sb("xs_l", [P, CH, P], F32R)
        hr_h, hr_l = sb("hr_h", [P, CH, P], F32R), sb("hr_l", [P, CH, P], F32R)
        ys = sb("ys", [P, 2, C])
        pick = sb("pick", [16, 4, P], F32R)
        home = sb("home", [P, 4], U32)
        homef = sb("homef", [P, 2])
        lg = part[:].rearrange("p a b -> p (a b)")[:, 0:NT * E].rearrange("p (t e) -> p t e", e=E)
        weight = sb("weight", [P, 2, NT])
        where = sb("where", [P, 2, NT], U32)
        where_pad = sb("where_pad", [P, E], U32)
        tile_ef = sb("tile_ef", [P, RT])
        tile_ei = sb("tile_ei", [1, RT // PACK], I32)
        tile_row = sb("tile_row", [16, RT])
        ysf = ys[:].rearrange("p a b -> p (a b)")
        mv = ysf[:, 0:2 * NT].rearrange("p (t a) -> p t a", a=2)
        rstd = ysf[:, 2 * NT:4 * NT].rearrange("p (a t) -> p a t", a=2)
        stats = ysf[:, 4 * NT:4 * NT + 6 * TT].rearrange("p (t a) -> p t a", a=6)

        with ExitStack() as place:
            wqkv_h, wqkv_l = (
                place.enter_context(nc.sbuf_tensor(name, [P, CH, 3 * C], F32R)) for name in ("wqkv_h", "wqkv_l"))
            w1_h, w1_l, w2_h, w2_l = (
                place.enter_context(nc.sbuf_tensor(name, [P, E + 1, CH, C], F32R))
                for name in ("w1_h", "w1_l", "w2_h", "w2_l"))
        EARLY_X = 2 * CH * 3 * C // (TT * C)
        comb_early, comb_y, comb_x = (
            sb(name, [P, n, k, C]) for name, n, k in (("comb_early", EARLY_X, TT), ("comb_y", SETS, 2 * TT),
                                                      ("comb_x", SETS - EARLY_X, TT)))

        def k(name):
            at, n = CONST[name]
            return cst[:, at:at + n]

        ident = k("ident")
        accf = acc[:].rearrange("p a b -> p (a b)")
        rk = [f[:, i * 256:(i + 1) * 256] for f, n in ((accf, 4), (part[:, 1, :], 2), (ysf, 2)) for i in range(n)]

        xt_f = [qkv[:, 0:CH, :], qkv[:, CH:2 * CH, :]]
        acc_rows = acc[:].rearrange("p c (t n) -> p (c t) n", n=C)
        xr = [acc_rows, qkv[:, 4:6, :].rearrange("p c (t n) -> p (c t) n", n=C)]
        sh_blind = [ys[:].rearrange("p a b -> p (a b)"), tile_in[:, ROW:ROW + 2 * C]]
        rows_f = rows[:].rearrange("p a b -> p (a b)")

        def shared_at(b, at, n):
            return rows_f[:, bass.ds(b * CH * T + at, n)]

        zpad = xs[:, 0, :]

        bank_d = [bank(f"bank_d{i}") for i in range(BANKS)]
        bank_s, bank_tx, bank_up, bank_th, bank_down = map(
            bank, ("bank_s", "bank_tx", "bank_up", "bank_th", "bank_down"))
        xt_bank = [bank_d[0:2], [bank_d[2], bank_th]]
        logit_bank = [bank_s, bank_up]

        x_in = [sem(f"x_in{i}") for i in range(B)]
        small_in = sem("small_in")
        raw_in = [sem(f"raw_in{i}") for i in range(STAGES)]
        hi_made, lo_early, lo_late = sem("hi_made"), sem("lo_early"), sem("lo_late")
        mv_done, rstd_done, pool_ve = sem("mv_done"), sem("rstd_done"), sem("pool_ve")
        xr_done, rows_done = sem("xr_done"), sem("rows_done")
        t_done, xt_done = sem("t_done"), sem("xt_done")
        logit_done, lg_done = sem("logit_done"), sem("lg_done")
        brow_in = sem("brow_in")
        rank_done, count_done, gap_done, exp_done = map(sem, ("rank_done", "count_done", "gap_done", "exp_done"))
        route_steps, route_done, pad_done, filled = map(
            sem, ("route_steps", "route_done", "pad_done", "filled"))
        scattered = sem("scattered")
        d_full = [sem(f"d_full{i}") for i in range(BANKS)]
        d_free = [sem(f"d_free{i}") for i in range(BANKS)]
        split_h, split_l = sem("split_h"), sem("split_l")
        prod_ready, prod_used = sem("prod_ready"), sem("prod_used")
        s_free, sums_out, s_full = map(sem, ("s_free", "sums_out", "s_full"))
        shifted, exped, normed, p_h, p_l = map(sem, ("shifted", "exped", "normed", "p_h", "p_l"))
        part_added = sem("part_added")
        mix_h, mix_l = sem("mix_h"), sem("mix_l")
        hs_h, hs_l, v_moved = sem("hs_h"), sem("hs_l"), sem("v_moved")
        sh_stored, sh_back = [sem("sh_stored0"), sem("sh_stored1")], sem("sh_back")
        xs_in = [sem("xs_in0"), sem("xs_in1")]
        tx_done, xs_hi, xs_lo = sem("tx_done"), sem("xs_hi"), sem("xs_lo")
        up_done, gelu_done = sem("up_done"), sem("gelu_done")
        th_done, hr_hi, hr_lo = sem("th_done"), sem("hr_hi"), sem("hr_lo")
        down_done, y_made = sem("down_done"), sem("y_made")
        y_out = [sem("y_out0"), sem("y_out1")]
        home_f, home_done, pick_done = sem("home_f"), sem("home_done"), sem("pick_done")
        dve_done = sem("dve_done")
        act_turn, pool_turn, sp_turn = map(sem, ("act_turn", "pool_turn", "sp_turn"))
        c_in = [sem(f"c_in{i}") for i in range(SETS)]
        g_parts, silu_done, sg_done = sem("g_parts"), sem("silu_done"), sem("sg_done")
        o_made = [sem(f"o_made{i}") for i in range(SETS)]
        c_out = [sem(f"c_out{i}") for i in range(SETS)]

        stage = [prod[:, i, :] for i in range(RING)] + [part[:, 1, :]]
        wq = w_qkv.rearrange("(c p) n -> p c n", p=P)
        dense_chunks = [(wq[:, :, h * C:(h + 1) * C], wqkv_h[:, :, h * C:(h + 1) * C], wqkv_l[:, :, h * C:(h + 1) * C])
                        for h in range(3)]
        dense_chunks += [(w_proj.rearrange("(c p) n -> p c n", p=P), wp_h[:], wp_l[:])]
        LOOPED = 2 * (E + 1)
        LOWS = STAGES + LOOPED

        def expert_chunk(g, j):
            e = bass.ds(g * 2 + j // 2, 1)
            raw, hi, lo = (w1, w1_h, w1_l) if j % 2 == 0 else (w2, w2_h, w2_l)
            return (raw[e].rearrange("a (c p) n -> p (a c) n", p=P),
                    hi[:, e].rearrange("p a c n -> p (a c) n"), lo[:, e].rearrange("p a c n -> p (a c) n"))

        def spread_chunk(j):
            return spread[:, j * 512:(j + 1) * 512], sp_r[:, 4 * j:4 * j + 4, :]

        def product_at(i):
            return prod[:, (i + 2) % RING, :]

        def staged(j, like):
            return stage[j].rearrange("p (c n) -> p c n", c=like.shape[1])

        def hold(eng, turn, s, v):
            eng.wait_ge(s, v)
            if turn is not None and not isinstance(v, int):
                eng.sem_inc(turn, 1)

        def drained(eng, turn, b, kind, i, j=0):
            k, n = bank_use(b, kind, i, j)
            hold(eng, turn, d_free[k], n + 2)

        def comb(n):
            co = qkv[:, 2 * n:2 * n + 2, :] if n < 3 else prod[:, 0:2, :]
            return (comb_early[:, n] if n < EARLY_X else comb_x[:, n - EARLY_X],
                    comb_y[:, n].rearrange("p t c -> p (t c)").rearrange("p (t c) -> p t c", t=TT),
                    co.rearrange("p a (t c) -> p (a t) c", c=C))

        block = ctx.enter_context(nc.Block())

        @block.sync
        def _(sp):
            for b in range(2):
                sp.dma_start(rows[:, b * TT:(b + 1) * TT, 0:C], x_b[b]).then_inc(x_in[b], 16)
            sp.dma_start(cst[:], consts).then_inc(small_in, 16)
            sp.dma_start(bqkv[:], b_qkv).then_inc(small_in, 16)
            sp.dma_start(bs1[:], sb1).then_inc(small_in, 16)
            sp.dma_start(gate[:], gate_t.rearrange("(c p) e -> p c e", p=P)).then_inc(small_in, 16)
            sp.dma_start(ebias[:], expert_bias.rearrange("(a e) -> a e", a=1).to_broadcast([P, E])).then_inc(small_in, 16)
            sp.dma_start(sco[0:16].rearrange("p a b c -> p (a b c)")[:, 0:256], bias_rows[:, 0:C]).then_inc(brow_in, 16)
            sp.dma_start(prb[0:16].rearrange("p a b c -> p (a b c)")[:, 0:256], bias_rows[:, C:2 * C]).then_inc(brow_in, 16)
            for b in range(2, B):
                sp.dma_start(rows[:, b * TT:(b + 1) * TT, 0:C], x_b[b]).then_inc(x_in[b], 16)
            for j, (src, hi, lo) in enumerate(dense_chunks):
                sp.dma_start(staged(j, src), src).then_inc(raw_in[j], 16)
            sp.wait_ge(pad_done, 2)
            sp.dma_start(slots_dram[2 * NT * P:, :].rearrange("(j p) c -> p j c", p=P),
                         zpad.rearrange("p (j c) -> p j c", j=1).to_broadcast([P, TAIL, ROW])).then_inc(filled, 16)
            sp.wait_ge(lo_early, STAGES)
            with sp.Fori(0, LOOPED // STAGES) as g:
                for j in range(STAGES):
                    hold(sp, sp_turn, lo_late, g * STAGES + j + 1)
                    src, hi, lo = expert_chunk(g, j)
                    sp.dma_start(staged(j, src), src).then_inc(raw_in[j], 16)
            for j in range(2):
                sp.wait_ge(lo_late, LOOPED + j + 1)
                sp.dma_start(stage[j], spread_chunk(j)[0]).then_inc(raw_in[j], 16)

            for b in range(BLIND):
                for i in range(2):
                    drained(sp, None, b, "shared_down", i)
                    sp.dma_start(shared_b[b, :, 2 * i:2 * i + 2, :], sh_blind[i].rearrange("p (t c) -> p t c", c=C))\
                        .then_inc(sh_stored[i], 16)
            sp.wait_ge(scattered, 16 * (2 * NT + E - 4))
            for n in range(2):
                sp.wait_ge(y_out[n], 32)
            for n in range(2):
                sp.wait_ge(sh_stored[n], 16 * BLIND)

            def load_tile(m, i):
                hold(sp, sp_turn, tx_done, m + 1)
                hold(sp, sp_turn, home_done, m + 1)
                sp.dma_start(xs[:, i % 2, :], slots_t[bass.ds(m, 1)].rearrange("a p c -> p (a c)"))\
                    .then_inc(xs_in[i % 2], 16)

            with sp.Fori(BLIND, B) as b:
                for kind, i in PLAN_ROUTED:
                    if kind == "tx":
                        load_tile((b - BLIND) * TILES_B + i, i)
            for b in range(BLIND):
                sp.dma_start(rows_f[:, b * CH * T:(b + 1) * CH * T].rearrange("p (t c) -> p t c", c=C), shared_b[b])\
                    .then_inc(sh_back, 16)

            drained(sp, None, B - 1, "qkv", 5)
            for b in range(EARLY_X):
                sp.dma_start(comb(b)[0], x_b[b]).then_inc(c_in[b], 16)
            for n in range(2):
                sp.wait_ge(y_out[n], 16 * (RT // 2 + 2))
            for b in range(B):
                n = b % SETS
                if b >= SETS:
                    sp.wait_ge(o_made[n], b // SETS + 1)
                cx, cy, co = comb(n)
                sp.dma_start(cy, routed_b[b]).then_inc(c_in[n], 16)
                if b >= EARLY_X:
                    sp.dma_start(cx, x_b[b]).then_inc(c_in[n], 16)
            for n in range(SETS):
                sp.wait_ge(c_out[n], 16 * (B // SETS + 1))

        @block.gpsimd
        def _(pool):
            pool.sem_inc(lo_late, STAGES)
            pool.memset(zpad[:], 0.0).then_inc(pad_done, 1)
            pool.wait_ge(pad_done, 1)
            pool.memset(zpad[:, C:C + 1], FAR).then_inc(pad_done, 1)
            pool.wait_ge(small_in, 80)
            for n in range(2):
                part_of = slice(n * (NT // 2), (n + 1) * (NT // 2))
                pool.wait_ge(mv_done, (n + 1) * (NT // 2))
                pool.tensor_scalar(rstd[:, 0, part_of], mv[:, part_of, 1], EPS, None, ALU.add).then_inc(pool_ve, 1)
                pool.wait_ge(pool_ve, n + 1)
                pool.tensor_tensor(rstd[:, 1, part_of], rstd[:, 0, part_of], k("minus_half")[:, part_of], ALU.pow)\
                    .then_inc(rstd_done, 1)
            with pool.Fori(0, LOOPED // STAGES) as g:
                for j in range(STAGES):
                    src, hi, lo = expert_chunk(g, j)
                    pool.wait_ge(hi_made, g * STAGES + (STAGES + j + 1))
                    pool.tensor_tensor(lo, staged(j, hi), hi.bitcast(F32), ALU.subtract).then_inc(lo_late, 1)
            pool.wait_ge(filled, 16)
            pool.wait_ge(rows_done, B)
            pool.wait_ge(route_done, 1)

            def to_slots(at, src, signal):
                pool.indirect_dma_start(slots_dram, bass.IndirectOffsetOnAxis(ap=at, axis=0), src, None,
                                        bounds_check=SLOTS - 1, oob_is_err=False).then_inc(signal, 16)

            for n in range(E):
                to_slots(where_pad[:, n:n + 1], zpad, y_out[n % 2] if n < 4 else scattered)
            for t in range(NT):
                for j in range(2):
                    to_slots(where[:, j, t:t + 1], rows[:, t, :], scattered)

            def batch(b):
                m0 = (b - BLIND) * TILES_B
                for kind, i in PLAN_ROUTED:
                    if kind == "turn":
                        pool.wait_ge(p_h, (b - i) * 2 + i + 1)
                        pool.tensor_tensor(phl[:, :, :, 1, :], prb[:], phl[:, :, :, 0, :].bitcast(F32),
                                           ALU.subtract).then_inc(p_l, 1)
                    if kind == "pv" and i % ND:
                        h, d = i // ND, i % ND
                        n = h * (ND - 1) + d - 1
                        lo = DIST[d]
                        if d == 1:
                            drained(pool, None, b, "pv", i - 1)
                        pool.wait_ge(part_added, (b - h) * ADDS + n + 2)
                        drained(pool, None, b, "pv", i)
                        pool.tensor_tensor(acc[:, h, lo:T], acc[:, h, lo:T], part[:, n % 2, lo:T],
                                           ALU.add).then_inc(part_added, 1)
                    if kind == "down":
                        m = m0 + i
                        pool.wait_ge(home_done, m + 3)
                        pool.wait_ge(y_made, m + 2)
                        pool.sem_inc(pool_turn, 1)
                        pool.indirect_dma_start(
                            routed_dram, bass.IndirectOffsetOnAxis(ap=home[:, i % 4:i % 4 + 1], axis=0),
                            ys[:, i % 2, :], None, bounds_check=2 * NT * P - 1, oob_is_err=False)\
                            .then_inc(y_out[i % 2], 16)

            with pool.Fori(BLIND, B) as b:
                batch(b)
            with pool.Fori(0, B // SETS) as g:
                for n in range(SETS):
                    b = g * SETS + n
                    cx, cy, co = comb(n)
                    pool.wait_ge(silu_done, b + 1)
                    pool.tensor_tensor(co, co, xnt[:, bass.ds(b, 1), :].rearrange("p a (t c) -> p (a t) c", c=C),
                                       ALU.mult).then_inc(sg_done, 1)
                    if n == 1:
                        pool.wait_ge(sg_done, b + 1)
                        pool.tensor_tensor(co, co, cx, ALU.add).then_inc(o_made[n], 1)

        @block.scalar
        def _(act):
            def wait(s, v):
                hold(act, act_turn, s, v)

            act.sem_inc(xt_done, 2 * CH * 2)
            act.sem_inc(gelu_done, 1)
            act.sem_inc(y_made, 1)
            for n in range(SETS):
                act.sem_inc(c_out[n], 16)
                act.sem_inc(o_made[n], 1)

            def transposed(g):
                for n in range(2):
                    b = g * 2 + n
                    wait(t_done, b * CH + 3 * CH)
                    wait(logit_done, b + 1)
                    for c in range(CH):
                        act.activation(xt_f[n][:, c, :], xt_bank[n][c][:], ACT.Copy).then_inc(xt_done, 1)
                    for c in range(CH):
                        act.activation(xnt[:, bass.ds(b, 1), c * T:(c + 1) * T].rearrange("p a n -> p (a n)"),
                                       xt_bank[n][c][:], ACT.Copy).then_inc(xt_done, 1)

            def expert_highs(g):
                for j in range(STAGES):
                    src, hi, lo = expert_chunk(g, j)
                    wait(raw_in[j], g * 16 + 32)
                    act.activation(hi, staged(j, hi), ACT.Copy).then_inc(hi_made, 1)

            transposed(0)
            for j, (src, hi, lo) in enumerate(dense_chunks):
                act.wait_ge(raw_in[j], 16)
                act.activation(hi, staged(j, hi), ACT.Copy).then_inc(hi_made, 1)
            expert_highs(0)
            with act.Fori(1, B // 2) as g:
                transposed(g)
                expert_highs(g)
            for j in range(2):
                hi = spread_chunk(j)[1]
                act.wait_ge(raw_in[j], 16 * (LOOPED // STAGES + 2))
                act.activation(hi, staged(j, hi), ACT.Copy).then_inc(hi_made, 1)

            def split(b):
                act.activation(t_h[:].rearrange("p c n -> p (c n)"),
                               xnt[:, bass.ds(b, 1), :].rearrange("p a n -> p (a n)"), ACT.Copy).then_inc(split_h, 1)

            def batch(b, routed):
                def full(kind, i, j=0):
                    k, n = bank_use(b, kind, i, j)
                    wait(d_full[k], n + 1)
                    return bank_d[k], d_free[k]

                m0 = (b - BLIND) * TILES_B
                for kind, i in plan_of(b, routed):
                    if kind == "route":
                        act.wait_ge(gap_done, 1)
                        act.activation(weight[:, 1, :], rk[7][:, 0:NT], ACT.Exp).then_inc(exp_done, 1)
                    if kind == "next_split":
                        split((b + 1) % B if isinstance(b, int) else (b + 1) & (B - 1))
                    if kind == "qkv":
                        half, which = divmod(i, 3)
                        src, free = full(kind, i)
                        act.activation(qkv[:, 6 if i == 5 else i, :], src[:], ACT.Identity,
                                       bias=bqkv[:, which * CH + half:which * CH + half + 1]).then_inc(free, 1)
                    if kind == "v_move":
                        drained(act, act_turn, b, "qkv", 5)
                        if not (isinstance(b, int) and b == 0):
                            drained(act, act_turn, b, "pv", 2 * ND - 1)
                        act.activation(qkv[:, 5, :], qkv[:, 6, :], ACT.Copy).then_inc(v_moved, 1)
                    if kind == "shared_up":
                        src, free = full(kind, i)
                        act.activation(hs[:, i, :], src[:], ACT.Gelu, bias=bs1[:, i:i + 1]).then_inc(free, 1)
                    if kind == "hs_split":
                        for j in range(2):
                            drained(act, act_turn, b, "shared_up", j)
                        act.activation(t_h[:], hs, ACT.Copy).then_inc(hs_h, 1)
                    if kind == "shared_down":
                        src, free = full(kind, i)
                        if not routed and b:
                            wait(sh_stored[i], 16 * b)
                        dst = shared_at(b, 2 * i * C, 2 * C) if routed else sh_blind[i]
                        act.activation(dst, src[:], ACT.Copy).then_inc(free, 1)
                    if kind == "score_turn":
                        wait(prod_used, b * 2 * ND + (i + 1) * ND + RING)
                        act.activation(score_t[0:ND * HH, :], bank_s[0:ND * HH, :], ACT.Copy).then_inc(sums_out, 1)
                    if kind == "soft_norm":
                        wait(shifted, (b - i) * 2 + i + 1)
                        act.activation(prb[:], sco[:], ACT.Exp, scale=SCALE).then_inc(exped, 1)
                    if kind == "turn":
                        wait(normed, (b - i) * 2 + i + 1)
                        act.activation(phl[:, :, :, 0, :], prb[:], ACT.Copy).then_inc(p_h, 1)
                        for j in range(2):
                            src, free = full(kind, i, j)
                            act.activation(turned[:, i, j, :], src[:], ACT.Copy).then_inc(free, 1)
                    if kind == "mix_split":
                        wait(part_added, b * ADDS + 2)
                        act.activation(t_h[:], acc[:], ACT.Copy).then_inc(mix_h, 1)
                    if kind == "project":
                        src, free = full(kind, i)
                        act.activation(xnt[:, bass.ds(b - 1, 1), i * T:(i + 1) * T].rearrange("p a n -> p (a n)"),
                                       src[:], ACT.Copy).then_inc(free, 1)
                    m = m0 + i
                    if kind == "tx":
                        wait(tx_done, m + 3)
                        wait(up_done, m + 1)
                        act.activation(xs_h[:].rearrange("p c n -> p (c n)"), bank_tx[:, 0:C], ACT.Copy).then_inc(xs_hi, 1)
                        if i % 2 == 0:
                            wait(down_done, m + 2)
                            act.activation(pick[:, i % 4:i % 4 + 2, :],
                                           tile_row[:, bass.ds(m, 2)].rearrange("p (a n) -> p a n", n=1).to_broadcast([16, 2, P]),
                                           ACT.Copy).then_inc(pick_done, 1)
                    if kind == "up":
                        wait(up_done, m + 2)
                        wait(th_done, m + 1)
                        act.activation(hr, bank_up[:, 0:C], ACT.Gelu).then_inc(gelu_done, 1)
                    if kind == "th":
                        wait(th_done, m + 2)
                        wait(down_done, m + 4)
                        act.activation(hr_h[:].rearrange("p c n -> p (c n)"), bank_th[:, 0:C], ACT.Copy).then_inc(hr_hi, 1)
                    if kind == "down":
                        wait(down_done, m + 5)
                        wait(y_out[i % 2], 16 * ((b - BLIND) * (TILES_B // 2) + i // 2 + 2))
                        act.activation(ys[:, i % 2, :], bank_down[:, 0:C], ACT.Copy).then_inc(y_made, 1)

            split(0)
            for b in range(BLIND):
                batch(b, False)
            act.wait_ge(scattered, 16 * (2 * NT + E - 4))
            for n in range(2):
                act.wait_ge(y_out[n], 32)
            for n in range(2):
                act.wait_ge(sh_stored[n], 16 * BLIND)
            with act.Fori(BLIND, B) as b:
                batch(b, True)
            batch(B, False)

            with act.Fori(0, B // SETS) as g:
                def store(n):
                    wait(o_made[n], g + 2)
                    act.dma_start(out_b[bass.ds(g * SETS + n, 1)].rearrange("a p t c -> p (a t) c"), comb(n)[2])\
                        .then_inc(c_out[n], 16)

                for n in range(SETS):
                    cx, cy, co = comb(n)
                    wait(g_parts, (g * SETS + n) * 8 + 8)
                    act.activation(co, co, ACT.Silu).then_inc(silu_done, 1)
                    if n:
                        store(n - 1)
                store(SETS - 1)

        @block.vector
        def _(dve):
            count = [0]

            def step(ins, base=None):
                count[0] += 1
                ins.then_inc(dve_done, 1)
                dve.wait_ge(dve_done, count[0] if base is None else base + count[0])

            dve.sem_inc(part_added, 2)
            dve.sem_inc(lg_done, 2)

            def mv_of(b, t, what):
                return mv[:, bass.ds(b * TT + t, 1), 0] if what == 0 else rstd[:, 1, bass.ds(b * TT + t, 1)]

            dve.wait_ge(small_in, 80)
            dve.wait_ge(brow_in, 32)
            for j, raw in enumerate((sco, prb)):
                r = raw[0:16].rearrange("p a b c -> p (a b c)")[:, 0:C]
                dst = brow[:, j * C:(j + 1) * C]
                tmp = part[0:16, 0, j * C:(j + 1) * C]
                step(dve.tensor_copy(dst, r))
                step(dve.tensor_tensor(tmp, r, dst.bitcast(F32), ALU.subtract))
                step(dve.tensor_scalar(tmp, tmp, k("row_lo")[0:16], None, ALU.mult))
                step(dve.scalar_tensor_tensor(dst, dst.bitcast(F32), k("row_hi")[0:16], tmp, ALU.mult, ALU.add))
            step(dve.tensor_scalar(part[0:16, 0, 0:P], k("ones")[0:16], k("row_expert")[0:16], None, ALU.mult))
            step(dve.tensor_scalar(dense_pick[:], part[0:16, 0, 0:P], -1.0, None, ALU.is_equal))
            before = count[0]

            def statistics(b):
                dve.wait_ge(x_in[b], 16)
                if b:
                    dve.wait_ge(mv_done, b * TT)
                for t in range(TT):
                    count[0] += 1
                    dve.bn_stats(stats[:, t, :], rows[:, b * TT + t, 0:C]).then_inc(dve_done, 1)
                dve.wait_ge(dve_done, count[0])
                for t in range(TT):
                    dve.bn_aggr(mv[:, b * TT + t, :], stats[:, t, :]).then_inc(mv_done, 1)

            def logits(b, n):
                dve.wait_ge(logit_done, b + 3)
                dve.tensor_tensor(lg[:, bass.ds(b * TT, TT), :],
                                  logit_bank[n][:, 0:TT * 8].rearrange("p (t e) -> p t e", e=8)[:, :, 0:E],
                                  ebias[:].rearrange("p (a e) -> p a e", a=1).to_broadcast([P, TT, E]), ALU.add)\
                    .then_inc(lg_done, 1)

            def row_tile(b, t):
                return rows[:, bass.ds(b * TT + t, 1), 0:C].rearrange("p a n -> p (a n)")

            def normalise(g):
                for n in range(2):
                    b = g * 2 + n
                    dve.wait_ge(t_done, b * CH + CH)
                    for t in range(TT):
                        dve.tensor_scalar(xr[n][:, t, :], row_tile(b, t), mv_of(b, t, 0), mv_of(b, t, 1),
                                          ALU.subtract, ALU.mult).then_inc(xr_done, 1)

            def normalise_in_place(g):
                for n in range(2):
                    b = g * 2 + n
                    dve.wait_ge(xr_done, b * TT + TT)
                    for t in range(TT):
                        ins = dve.tensor_scalar(row_tile(b, t), row_tile(b, t), mv_of(b, t, 0), mv_of(b, t, 1),
                                                ALU.subtract, ALU.mult)
                    ins.then_inc(rows_done, 1)

            for b in range(AHEAD):
                statistics(b)
            dve.wait_ge(rstd_done, 1)
            normalise(0)
            for b in range(AHEAD, B):
                statistics(b)
            normalise_in_place(0)
            for j, (src, hi, lo) in enumerate(dense_chunks):
                dve.wait_ge(hi_made, j + 1)
                dve.tensor_tensor(lo, staged(j, hi), hi.bitcast(F32), ALU.subtract).then_inc(lo_early, 1)
            dve.wait_ge(rstd_done, 2)
            with dve.Fori(1, B // 2) as g:
                normalise(g)
                for n in range(2):
                    logits(g * 2 - 2 + n, n)
                normalise_in_place(g)
            for n in range(2):
                logits(B - 2 + n, n)

            base_n = count[0]

            routed_steps = [0]

            def route_step(ins):
                routed_steps[0] += 1
                ins.then_inc(route_steps, 1)
                dve.wait_ge(route_steps, routed_steps[0])

            def route():
                dve.wait_ge(lg_done, B + 2)
                dve.wait_ge(rows_done, B)
                dve.wait_ge(lo_late, LOWS)
                dve.wait_ge(hi_made, LOWS + 2)

                def te(a):
                    return a[:, 0:NT * E].rearrange("p (t e) -> p t e", e=E)

                def row_e(a):
                    return a.rearrange("p (a e) -> p a e", a=1).to_broadcast([P, NT, E])

                rank, win, sel1, sel2, slot, tmp, total = map(te, rk[0:7])
                small = rk[7]
                route_step(dve.tensor_copy(rank, row_e(k("rank0"))))
                for s in range(1, E):
                    route_step(dve.tensor_tensor(win[:, :, 0:E - s], lg[:, :, 0:E - s], lg[:, :, s:E], ALU.is_ge))
                    route_step(dve.tensor_tensor(rank[:, :, s:E], rank[:, :, s:E], win[:, :, 0:E - s], ALU.add))
                    route_step(dve.tensor_tensor(rank[:, :, 0:E - s], rank[:, :, 0:E - s], win[:, :, 0:E - s], ALU.subtract))
                route_step(dve.tensor_scalar(sel1, rank, 0.0, None, ALU.is_equal))
                route_step(dve.tensor_scalar(sel2, rank, 1.0, None, ALU.is_equal))
                dve.tensor_tensor(win, sel1, sel2, ALU.add).then_inc(rank_done, 1)
                dve.wait_ge(rank_done, 1)
                route_step(dve.tensor_tensor(tmp, sel2, lg, ALU.mult))
                route_step(dve.tensor_reduce(weight[:, 1, :], tmp, AX.X, ALU.add))
                route_step(dve.tensor_reduce(weight[:, 0, :], lg, AX.X, ALU.max))
                dve.tensor_tensor(small[:, 0:NT], weight[:, 1, :], weight[:, 0, :], ALU.subtract).then_inc(gap_done, 1)
                route_step(dve.tensor_tensor(tmp, sel1, row_e(k("expert")), ALU.mult))
                route_step(dve.tensor_reduce(rows[:, :, C + 1:C + 2].rearrange("p t a -> p (t a)"), tmp, AX.X, ALU.add))
                route_step(dve.tensor_copy(rows[:, :, C:C + 1].rearrange("p t a -> p (t a)"), k("token2")))
                dve.wait_ge(count_done, 2)
                route_step(dve.tensor_copy(total, te(bank_tx)))
                for e in range(E):
                    route_step(dve.tensor_tensor_scan(tmp[:, :, e], k("ones")[:, 0:NT], total[:, :, e], 0.0, ALU.mult, ALU.add))
                cnt = small[:, 32:32 + E]
                tiles = small[:, 40:40 + E]
                end = small[:, 48:48 + E]
                base = small[:, 56:56 + E]
                over = small[:, 64:64 + E]
                pad = small[:, 80:80 + E]
                route_step(dve.tensor_copy(cnt, tmp[:, NT - 1, :]))
                route_step(dve.tensor_tensor(slot, tmp, total, ALU.subtract))
                route_step(dve.tensor_tensor(slot, slot, te(bank_s), ALU.add))
                et = rk[1][:, 0:E * NT].rearrange("p (e t) -> p e t", t=NT)
                route_step(dve.tensor_tensor(et, cnt.rearrange("p (e a) -> p e a", a=1).to_broadcast([P, E, NT]),
                                       k("edges").rearrange("p (a t) -> p a t", a=1).to_broadcast([P, E, NT]), ALU.is_gt))
                route_step(dve.tensor_reduce(tiles, et, AX.X, ALU.add))
                route_step(dve.tensor_tensor_scan(end, k("ones")[:, 0:E], tiles, 0.0, ALU.mult, ALU.add))
                route_step(dve.tensor_tensor(base, end, tiles, ALU.subtract))
                route_step(dve.tensor_scalar(base, base, float(P), None, ALU.mult))
                route_step(dve.tensor_tensor(slot, slot, row_e(base), ALU.add))
                for j, sel in enumerate((sel1, sel2)):
                    route_step(dve.tensor_tensor(tmp, sel, slot, ALU.mult))
                    route_step(dve.tensor_reduce(rk[1][:, j * NT:(j + 1) * NT], tmp, AX.X, ALU.add))
                    route_step(dve.tensor_copy(where[:, j, :], rk[1][:, j * NT:(j + 1) * NT]))
                je = prod[:, 2, 0:RT * E].rearrange("p (j e) -> p j e", e=E)
                route_step(dve.tensor_tensor(je, k("tile_no").rearrange("p (j a) -> p j a", a=1).to_broadcast([P, RT, E]),
                                       end.rearrange("p (a e) -> p a e", a=1).to_broadcast([P, RT, E]), ALU.is_ge))
                route_step(dve.tensor_reduce(tile_ef[:], je, AX.X, ALU.add))
                route_step(dve.tensor_scalar(tile_ef[:], tile_ef[:], float(E - 1), None, ALU.min))
                packed = rk[0][0:1, 0:RT].rearrange("p (a n) -> p a n", n=PACK)
                route_step(dve.tensor_tensor(packed, tile_ef[0:1, :].rearrange("p (a n) -> p a n", n=PACK),
                                       k("octal")[0:1].rearrange("p (a n) -> p a n", a=1).to_broadcast([1, RT // PACK, PACK]),
                                       ALU.mult))
                route_step(dve.tensor_reduce(rk[0][0:1, 128:128 + RT // PACK], packed, AX.X, ALU.add))
                route_step(dve.tensor_copy(tile_ei[:], rk[0][0:1, 128:128 + RT // PACK]))
                route_step(dve.tensor_scalar(tile_row[:], tile_ef[0:16, :], k("row_expert")[0:16], None, ALU.is_equal))
                route_step(dve.tensor_scalar(end, end, float(P), None, ALU.mult))
                route_step(dve.tensor_tensor(pad, base, cnt, ALU.add))
                route_step(dve.tensor_scalar(pad, pad, k("lane"), None, ALU.add))
                route_step(dve.tensor_tensor(over, pad, end, ALU.is_ge))
                route_step(dve.scalar_tensor_tensor(pad, over, FAR, pad, ALU.mult, ALU.add))
                route_step(dve.tensor_copy(where_pad[:], pad))
                dve.wait_ge(exp_done, 1)
                route_step(dve.tensor_scalar(small[:, 0:NT], weight[:, 1, :], 1.0, None, ALU.add))
                route_step(dve.reciprocal(weight[:, 0, :], small[:, 0:NT]))
                dve.tensor_tensor(weight[:, 1, :], weight[:, 1, :], weight[:, 0, :], ALU.mult).then_inc(route_done, 1)
                dve.wait_ge(route_done, 1)
                dve.sem_inc(s_free, 1)

            def split(b):
                dve.tensor_tensor(t_l[:].rearrange("p c n -> p (c n)"),
                                  xnt[:, bass.ds(b, 1), :].rearrange("p a n -> p (a n)"),
                                  t_h[:].rearrange("p c n -> p (c n)").bitcast(F32), ALU.subtract).then_inc(split_l, 1)

            def batch(b, routed, first, per, start):
                count[0] = 0
                origin = start + b * per + (0 if isinstance(b, int) and b == 0 else first - per)

                def mark(ins):
                    step(ins, origin)

                def full(kind, i):
                    k, n = bank_use(b, kind, i)
                    dve.wait_ge(d_full[k], n + 1)
                    return bank_d[k], d_free[k]

                m0 = (b - BLIND) * TILES_B
                for kind, i in plan_of(b, routed):
                    m = m0 + i
                    if kind == "route":
                        route()
                    if kind == "next_split":
                        dve.wait_ge(split_h, b + 2)
                        split((b + 1) % B if isinstance(b, int) else (b + 1) & (B - 1))
                    if kind == "product":
                        h, d = divmod(i, ND)
                        if i == 1:
                            dve.wait_ge(hs_l, b + 1)
                        if d == 0:
                            for j in range(2):
                                drained(dve, None, b, "qkv", 3 * h + j)
                        lo = DIST[d]
                        dve.wait_ge(prod_used, b * 2 * ND + max(i + 1, RING))
                        dve.tensor_tensor(product_at(i)[:, lo:T], qkv[:, 3 * h, lo:T], qkv[:, 3 * h + 1, 0:T - lo],
                                          ALU.mult).then_inc(prod_ready, 1)
                    if kind == "soft_max":
                        dve.wait_ge(s_full, b * 2 + i + 1)
                        s4 = bank_s[:, 0:TT * ND * HH].rearrange("p (t d h) -> p t d h", d=ND, h=HH)
                        msk = k("mask").rearrange("p (t d a) -> p t d a", d=ND, a=1).to_broadcast([P, TT, ND, HH])
                        dve.tensor_tensor(sco[:], s4, msk, ALU.add).then_inc(s_free, 1)
                        dve.wait_ge(s_free, b * 2 + i + 2)
                        mark(dve.tensor_reduce(red[:, 0], sco[:].rearrange("p t d h -> p t h d"), AX.X, ALU.max))
                        dve.tensor_tensor(sco[:], sco[:],
                                          red[:, 0:1].rearrange("p a t h -> p t a h").to_broadcast([P, TT, ND, HH]),
                                          ALU.subtract).then_inc(shifted, 1)
                    if kind == "soft_norm":
                        dve.wait_ge(exped, (b - i) * 2 + i + 1)
                        mark(dve.tensor_reduce(red[:, 1], prb[:].rearrange("p t d h -> p t h d"), AX.X, ALU.add))
                        mark(dve.reciprocal(red[:, 2], red[:, 1]))
                        dve.tensor_tensor(prb[:], prb[:],
                                          red[:, 2:3].rearrange("p a t h -> p t a h").to_broadcast([P, TT, ND, HH]),
                                          ALU.mult).then_inc(normed, 1)
                    if kind == "turn" and not routed:
                        dve.wait_ge(p_h, (b - i) * 2 + i + 1)
                        dve.tensor_tensor(phl[:, :, :, 1, :], prb[:], phl[:, :, :, 0, :].bitcast(F32),
                                          ALU.subtract).then_inc(p_l, 1)
                    if kind == "hs_split":
                        dve.wait_ge(hs_h, b + 1)
                        dve.tensor_tensor(t_l[:], hs, t_h[:].bitcast(F32), ALU.subtract).then_inc(hs_l, 1)
                    if kind == "pv":
                        h, d = i // ND, i % ND
                        lo = DIST[d]
                        src, free = full(kind, i)
                        if d == 0:
                            if h == 0:
                                dve.wait_ge(mix_l, b + 1)
                                drained(dve, None, b, "qkv", 2)
                            else:
                                dve.wait_ge(v_moved, b)
                            dve.tensor_tensor(acc[:, h, :], src[:], qkv[:, 3 * h + 2, :], ALU.mult).then_inc(free, 1)
                        else:
                            n = h * (ND - 1) + d - 1
                            dve.wait_ge(part_added, (b - h) * ADDS + n + 1)
                            at = lo % 2
                            dve.tensor_tensor(part[:, n % 2, lo:T], src[:, at:at + T - lo], qkv[:, 3 * h + 2, 0:T - lo],
                                              ALU.mult).then_inc(free, 1)
                        for j in range(max(i - 1, ND * h + 1), i if d < ND - 1 else i + 1) if not routed else ():
                            n, lo = h * (ND - 1) + j % ND - 1, DIST[j % ND]
                            if j % ND == 1:
                                drained(dve, None, b, "pv", j - 1)
                            dve.wait_ge(part_added, (b - h) * ADDS + n + 2)
                            drained(dve, None, b, "pv", j)
                            dve.tensor_tensor(acc[:, h, lo:T], acc[:, h, lo:T], part[:, n % 2, lo:T],
                                              ALU.add).then_inc(part_added, 1)
                    if kind == "mix_split":
                        dve.wait_ge(mix_h, b)
                        dve.tensor_tensor(t_l[:], acc[:], t_h[:].bitcast(F32), ALU.subtract).then_inc(mix_l, 1)
                    if kind == "tx":
                        dve.wait_ge(xs_in[i % 2], 16 * ((b - BLIND) * (TILES_B // 2) + i // 2 + 1))
                        dve.wait_ge(home_done, m + 2)
                        dve.tensor_tensor(homef[:, 0:1], xs[:, i % 2, C + 1:C + 2], tile_ef[:, bass.ds(m, 1)],
                                          ALU.not_equal).then_inc(home_f, 1)
                        dve.wait_ge(home_f, m + 1)
                        dve.wait_ge(y_out[i % 2], 16 * ((b - BLIND) * (TILES_B // 2) + i // 2 + 1))
                        dve.tensor_tensor(home[:, i % 4:i % 4 + 1], homef[:, 0:1], xs[:, i % 2, C:C + 1],
                                          ALU.add).then_inc(home_done, 1)
                        dve.wait_ge(xs_hi, m + 1)
                        dve.tensor_tensor(xs_l[:].rearrange("p c n -> p (c n)"), bank_tx[:, 0:C],
                                          xs_h[:].rearrange("p c n -> p (c n)").bitcast(F32), ALU.subtract)\
                            .then_inc(xs_lo, 1)
                    if kind == "th":
                        dve.wait_ge(hr_hi, m + 1)
                        dve.tensor_tensor(hr_l[:].rearrange("p c n -> p (c n)"), bank_th[:, 0:C],
                                          hr_h[:].rearrange("p c n -> p (c n)").bitcast(F32), ALU.subtract)\
                            .then_inc(hr_lo, 1)
                return count[0]

            dve.sem_inc(home_done, 2)
            dve.sem_inc(xs_lo, 1)
            dve.sem_inc(hr_lo, 1)
            dve.sem_inc(mix_l, 1)
            first, per = 2 + 2, 3 + 3
            dve.wait_ge(split_h, 1)
            split(0)
            for b in range(BLIND):
                assert batch(b, False, first, per, base_n) == (per if b else first)
            with dve.Fori(BLIND, B) as b:
                assert batch(b, True, first, per, base_n) == per
            batch(B, False, first, per, base_n)

            dve.wait_ge(sh_back, 16 * BLIND)
            with dve.Fori(0, B // SETS) as g:
                def add(n):
                    cx, cy, co = comb(n)
                    dve.wait_ge(sg_done, g * SETS + n + 1)
                    dve.tensor_tensor(co, co, cx, ALU.add).then_inc(o_made[n], 1)

                for n in range(SETS):
                    b = g * SETS + n
                    cx, cy, co = comb(n)
                    dve.wait_ge(c_out[n], g * 16 + 16)
                    dve.wait_ge(c_in[n], g * 32 + 32)
                    for j in range(2):
                        for t in range(TT):
                            w = weight[:, j, bass.ds(b * TT + t, 1)]
                            y = cy[:, t, j * C:(j + 1) * C]
                            other = shared_at(b, t * C, C) if j == 0 else co[:, t, :]
                            dve.scalar_tensor_tensor(co[:, t, :], y, w, other, ALU.mult, ALU.add).then_inc(g_parts, 1)
                        dve.wait_ge(g_parts, b * 8 + j * 4 + 4)
                    if n in (1, 3):
                        add(n - 1)
                add(SETS - 1)

        @block.tensor
        def _(pe):
            for i in range(BANKS):
                pe.sem_inc(d_free[i], 1)
            pe.sem_inc(logit_done, 2)
            pe.sem_inc(t_done, 2 * CH)
            pe.sem_inc(prod_used, RING)
            pe.sem_inc(tx_done, 2)
            pe.sem_inc(up_done, 1)
            pe.sem_inc(th_done, 1)
            pe.sem_inc(down_done, 4)
            pe.wait_ge(small_in, 80)
            with pe.Fori(0, B // 2) as g:
                for n in range(2):
                    b = g * 2 + n
                    pe.wait_ge(xr_done, b * TT + TT)
                    pe.wait_ge(xt_done, b * 2 * CH + 2 * CH)
                    for c in range(CH):
                        for t in range(TT):
                            last = pe.transpose(xt_bank[n][c][:, t * P:(t + 1) * P], xr[n][:, t, c * P:(c + 1) * P],
                                                ident)
                        last.then_inc(t_done, 1)
                for n in range(2):
                    b = g * 2 + n
                    pe.wait_ge(xt_done, b * 2 * CH + 4 * CH + CH)
                    pe.wait_ge(lg_done, b + 1)
                    for t in range(TT):
                        for c in range(CH):
                            last = pe.matmul(logit_bank[n][:, t * 8:t * 8 + E], xt_f[n][:, c, t * P:(t + 1) * P],
                                             gate[:, c, :], start=c == 0, stop=c == CH - 1)
                    last.then_inc(logit_done, 1)
            pe.wait_ge(xt_done, B * 2 * CH + 4 * CH)
            pe.wait_ge(lo_early, STAGES)
            pe.wait_ge(lo_late, LOWS)
            pe.wait_ge(hi_made, LOWS + 2)

            def three(dst, left, right, first=True, last=True):
                n = 0
                for c in range(CH):
                    for a, w in ((0, 0), (0, 1), (1, 0)):
                        mm = pe.matmul(dst, left[a](c), right[w](c), start=first and n == 0,
                                       stop=last and n == 3 * CH - 1)
                        n += 1
                return mm

            def batch(b, routed):
                def take(kind, i, j=0):
                    k, n = bank_use(b, kind, i, j)
                    pe.wait_ge(d_free[k], n + 1)
                    return bank_d[k], d_full[k]

                m0 = (b - BLIND) * TILES_B
                experts = []
                for a in range(TILES_B // PACK if routed else 0):
                    packed = pe.value_load(tile_ei[0:1, bass.ds((b - BLIND) * (TILES_B // PACK) + a, 1)],
                                           min_val=0, max_val=8 ** PACK - 1)
                    experts += [pe.snap((packed >> (3 * i)) & 7) for i in range(PACK)]
                for kind, i in plan_of(b, routed):
                    m = m0 + i
                    if kind == "route":
                        pe.wait_ge(rank_done, 1)
                        win = rk[1][:, 0:NT * E]
                        pe.matmul(bank_s[:, 0:NT * E], k("before"), win, start=True, stop=True).then_inc(count_done, 1)
                        pe.matmul(bank_tx[:, 0:NT * E], k("ones"), win, start=True, stop=True).then_inc(count_done, 1)
                    if kind == "qkv":
                        half, which = divmod(i, 3)
                        col = which * C + half * P
                        dst, fullsem = take(kind, i)
                        three(dst[:], [lambda c: wqkv_h[:, c, col:col + P], lambda c: wqkv_l[:, c, col:col + P]],
                              [lambda c: t_h[:, c, :], lambda c: t_l[:, c, :]]).then_inc(fullsem, 1)
                    if kind == "shared_up":
                        if i == 0:
                            pe.wait_ge(split_l, b + 1)
                        dst, fullsem = take(kind, i)
                        s = slice(i * P, (i + 1) * P)
                        three(dst[:], [lambda c: w1_h[:, SHARED, c, s], lambda c: w1_l[:, SHARED, c, s]],
                              [lambda c: t_h[:, c, :], lambda c: t_l[:, c, :]]).then_inc(fullsem, 1)
                    if kind in ("shared_down", "project"):
                        dst, fullsem = take(kind, i)
                        if kind == "project":
                            pe.wait_ge(mix_l, b + 1)
                            wh, wl = (lambda c: wp_h[:, c, :]), (lambda c: wp_l[:, c, :])
                        else:
                            pe.wait_ge(hs_l, b + 1)
                            wh, wl = (lambda c: w2_h[:, SHARED, c, :]), (lambda c: w2_l[:, SHARED, c, :])
                        bias = brow[:, 0:C] if kind == "project" else brow[:, C:2 * C]
                        for j in range(2):
                            s = slice((2 * i + j) * P, (2 * i + j + 1) * P)
                            o = dst[:, j * C:(j + 1) * C]
                            three(o, [lambda c: t_h[:, c, s], lambda c: t_l[:, c, s]], [wh, wl], last=False)
                            mm = pe.matmul(o, dense_pick[:], bias, start=False, stop=True)
                        mm.then_inc(fullsem, 1)
                    if kind == "score":
                        h, d = divmod(i, ND)
                        if d == 0:
                            pe.wait_ge(s_free, b * 2 + h + 1)
                        pe.wait_ge(prod_ready, b * 2 * ND + i + 1)
                        lo = DIST[d]
                        at = (ND - 1 - d) * HH
                        pe.matmul(bank_s[0:ND * HH, lo:T], k("head_sum")[:, at:at + ND * HH],
                                  product_at(i)[:, lo:T], start=d == 0, stop=d == ND - 1).then_inc(prod_used, 1)
                    if kind == "score_turn":
                        pe.wait_ge(sums_out, b * 2 + i + 1)
                        for t in range(TT):
                            at = t * ND * HH
                            mm = pe.transpose(bank_s[:, at:at + ND * HH], score_t[0:ND * HH, t * P:(t + 1) * P],
                                              ident[0:ND * HH, 0:ND * HH])
                        mm.then_inc(s_full, 1)
                    if kind == "turn":
                        pe.wait_ge(p_l, (b - i) * 2 + i + 1)
                        flat = phl[:].rearrange("p t d a h -> p t (d a h)").bitcast(F32)
                        for j in range(2):
                            dst, fullsem = take(kind, i, j)
                            n0 = (0, SECOND * 2 * HH)[j]
                            for t in range(TT):
                                mm = pe.transpose(dst[:, t * P:(t + 1) * P], flat[:, t, n0:n0 + P], ident)
                            mm.then_inc(fullsem, 1)
                    if kind == "pv":
                        h, d = i // ND, i % ND
                        if d == 0:
                            for j in range(2):
                                drained(pe, None, b, "turn", h, j)
                        dst, fullsem = take(kind, i)
                        lo = DIST[d] // 2 * 2
                        j, pick_d = (0, d) if d < 8 else (1, d - SECOND)
                        pe.matmul(dst[:, 0:T - lo], sp_r[:, pick_d, :], turned[:, h, j, lo:T], start=True, stop=True)\
                            .then_inc(fullsem, 1)
                    if kind == "tx":
                        pe.wait_ge(xs_in[i % 2], 16 * ((b - BLIND) * (TILES_B // 2) + i // 2 + 1))
                        pe.wait_ge(xs_lo, m + 1)
                        for c in range(CH):
                            mm = pe.transpose(bank_tx[:, c * P:(c + 1) * P], xs[:, i % 2, c * P:(c + 1) * P], ident)
                        mm.then_inc(tx_done, 1)
                    if kind == "th":
                        pe.wait_ge(gelu_done, m + 2)
                        pe.wait_ge(hr_lo, m + 1)
                        for c in range(CH):
                            mm = pe.transpose(bank_th[:, c * P:(c + 1) * P], hr[:, c * P:(c + 1) * P], ident)
                        mm.then_inc(th_done, 1)
                    if kind in ("up", "down"):
                        up = kind == "up"
                        e = experts[i]
                        l_h, l_l = (xs_h, xs_l) if up else (hr_h, hr_l)
                        r_h, r_l = (w1_h, w1_l) if up else (w2_h, w2_l)
                        o = (bank_up if up else bank_down)[:, 0:C]
                        if up:
                            pe.wait_ge(pick_done, (b - BLIND) * (TILES_B // 2) + i // 2 + 1)
                            pe.wait_ge(xs_lo, m + 2)
                            pe.wait_ge(gelu_done, m + 1)
                        else:
                            pe.wait_ge(hr_lo, m + 2)
                            pe.wait_ge(y_made, m + 1)
                        pe.matmul(o, pick[:, i % 4, :], brow[:, 0:C] if up else brow[:, C:2 * C], start=True, stop=False)

                        def moving(r):
                            return lambda c: r[:, bass.ds(e, 1), c, :].rearrange("p a n -> p (a n)")
                        three(o, [lambda c: l_h[:, c, :], lambda c: l_l[:, c, :]], [moving(r_h), moving(r_l)],
                              first=False).then_inc(up_done if up else down_done, 1)

            for b in range(BLIND):
                batch(b, False)
            pe.wait_ge(route_done, 1)
            with pe.Fori(BLIND, B) as b:
                batch(b, True)
            batch(B, False)


def kernel(L0_attn_x, L0_attn_W_qkv, L0_attn_b_qkv, L0_attn_W_proj, L0_attn_b_proj, L0_ffn_gate_w,
           L0_ffn_expert_bias, L0_ffn_sw1, L0_ffn_sb1, L0_ffn_sw2, L0_ffn_sb2, L0_ffn_rw1, L0_ffn_rb1,
           L0_ffn_rw2, L0_ffn_rb2):
    import concourse.bacc as bacc
    from concourse.bass_utils import run_bass_kernel_spmd

    a = {k: np.asarray(v) for k, v in dict(
        x=L0_attn_x, w_qkv=L0_attn_W_qkv, w_proj=L0_attn_W_proj, expert_bias=L0_ffn_expert_bias).items()}
    a["b_qkv"] = np.asarray(L0_attn_b_qkv).reshape(-1, P).T
    a["sb1"] = np.asarray(L0_ffn_sb1).reshape(-1, P).T
    a["gate_t"] = np.asarray(L0_ffn_gate_w).T
    a["w1"] = np.concatenate([np.asarray(L0_ffn_rw1), np.asarray(L0_ffn_sw1)[None]])
    a["w2"] = np.concatenate([np.asarray(L0_ffn_rw2), np.asarray(L0_ffn_sw2)[None]])
    routed = np.concatenate([np.asarray(L0_ffn_rb1), np.asarray(L0_ffn_rb2)], axis=1)
    dense = np.concatenate([np.asarray(L0_attn_b_proj), np.asarray(L0_ffn_sb2)])[None]
    a["bias_rows"] = np.concatenate([routed, routed, dense, dense])
    a["consts"], a["spread"] = constants()

    nc = bacc.Bacc("TRN2", target_bir_lowering=False, num_devices=1, dynamic_dma_scratch_size=7168)
    arrays, args = {}, {}
    for name, v in a.items():
        arrays[f"in_{name}"] = np.ascontiguousarray(v)
        args[name] = nc.dram_tensor(f"in_{name}", v.shape, F32, kind="ExternalInput").ap()
    args["out"] = nc.dram_tensor("out_x", (B, T, C), F32, kind="ExternalOutput").ap()
    args["slots_dram"] = nc.dram_tensor("slots", (SLOTS, ROW), F32, kind="Internal").ap()
    args["routed_dram"] = nc.dram_tensor("routed", (2 * B * T, C), F32, kind="Internal").ap()
    args["shared_dram"] = nc.dram_tensor("shared", (B * T, C), F32, kind="Internal").ap()
    build(nc, **args)
    r = run_bass_kernel_spmd(nc, [arrays], core_ids=[0])
    return r.results[0]["out_x"]
```
